# Optimizing a Trainium2 kernel written in Bass

```python
import numpy as np
import jax
import jax.numpy as jnp

def _softmax(x, axis=-1):
    return jax.nn.softmax(x, axis=axis)

def _gelu(x):
    return jax.nn.gelu(x, approximate=True)

def _silu(x):
    return jax.nn.silu(x)

def _sigmoid(x):
    return jax.nn.sigmoid(x)

def _layernorm(x, axis=-1, eps=1e-05):
    m = jnp.mean(x, axis=axis, keepdims=True)
    v = jnp.var(x, axis=axis, keepdims=True)
    return (x - m) / jnp.sqrt(v + eps)

def _scatter_add(tgt, idx, src, axis=0):
    return tgt.at[idx].add(src)

def _segment_sum(src, seg, n):
    return jax.ops.segment_sum(src, seg, n)
kernel_name = 'mk_gnn_preln_d1_gnn_r8_e717e5'

def setup_inputs(seed: int=0):
    np.random.seed(seed)
    _w = jnp.asarray

    def _rec_inputs():
        import jax
        import jax.numpy as jnp
        _gk = jax.random.key(seed)
        x = -0.0003713 + 1 * jax.random.normal(jax.random.fold_in(_gk, 1), (6250, 128), jnp.float32)
        _s = jax.random.randint(jax.random.fold_in(_gk, 2), (100000,), 0, 6250, jnp.int32)
        _d = jax.random.randint(jax.random.fold_in(_gk, 3), (100000,), 0, 6250, jnp.int32)
        _loop = jnp.arange(6250, dtype=jnp.int32)
        src = jnp.concatenate([_s, _d, _loop])
        dst = jnp.concatenate([_d, _s, _loop])
        _o = jnp.argsort(dst, stable=True)
        src = src[_o]
        dst = dst[_o]
        edge_attr_64 = 0.000155561 + 1.00019 * jax.random.normal(jax.random.fold_in(_gk, 11), (206250, 64), jnp.float32)
        return (x, src, dst, edge_attr_64)
    x, src, dst, edge_attr_64 = _rec_inputs()

    def _L0_gnn_setup():
        import jax, jax.numpy as jnp
        import numpy as np
        N, E, D, ED = (12500, 75000, 128, 64)
        RMS_EPS = 1.1920929e-07
        DEG_POWER = 0.5
        key = jax.random.key(seed)
        ks = jax.random.split(key, 12)
        s = 0.05
        return {'x': jax.random.normal(ks[0], (N, D), jnp.float32), 'edge_index': jax.random.randint(ks[1], (2, E), 0, N, jnp.int32), 'edge_attr': jax.random.normal(ks[2], (E, ED), jnp.float32), 'W1n': jax.random.normal(ks[3], (D, D), jnp.float32) * s, 'b1n': jnp.zeros((D,), jnp.float32), 'W2n': jax.random.normal(ks[4], (D, D), jnp.float32) * s, 'b2n': jnp.zeros((D,), jnp.float32), 'W1e': jax.random.normal(ks[5], (ED, D), jnp.float32) * s, 'b1e': jnp.zeros((D,), jnp.float32), 'W2e': jax.random.normal(ks[6], (D, D), jnp.float32) * s, 'b2e': jnp.zeros((D,), jnp.float32), 'gin_eps': jnp.float32(0.0), 'rms_w': jnp.ones((D,), jnp.float32)}
    _L0_gnn_all = _L0_gnn_setup()
    _L0_gnn_in = {k: v for k, v in _L0_gnn_all.items() if k in ('W1n', 'b1n', 'W2n', 'b2n', 'W1e', 'b1e', 'W2e', 'b2e', 'gin_eps', 'rms_w')}
    del _L0_gnn_all
    return {'x': x, 'src': src, 'dst': dst, 'edge_attr_64': edge_attr_64, 'L0_gnn_W1n': _L0_gnn_in['W1n'], 'L0_gnn_b1n': _L0_gnn_in['b1n'], 'L0_gnn_W2n': _L0_gnn_in['W2n'], 'L0_gnn_b2n': _L0_gnn_in['b2n'], 'L0_gnn_W1e': _L0_gnn_in['W1e'], 'L0_gnn_b1e': _L0_gnn_in['b1e'], 'L0_gnn_W2e': _L0_gnn_in['W2e'], 'L0_gnn_b2e': _L0_gnn_in['b2e'], 'L0_gnn_gin_eps': _L0_gnn_in['gin_eps'], 'L0_gnn_rms_w': _L0_gnn_in['rms_w']}

def reference(x, src, dst, edge_attr_64, L0_gnn_W1n, L0_gnn_b1n, L0_gnn_W2n, L0_gnn_b2n, L0_gnn_W1e, L0_gnn_b1e, L0_gnn_W2e, L0_gnn_b2e, L0_gnn_gin_eps, L0_gnn_rms_w):
    import jax
    import jax.numpy as jnp

    def _L0_gnn_ref(x, edge_index, edge_attr, W1n, b1n, W2n, b2n, W1e, b1e, W2e, b2e, gin_eps, rms_w):
        import jax, jax.numpy as jnp
        import numpy as np
        N, E, D, ED = (12500, 75000, 128, 64)
        RMS_EPS = 1.1920929e-07
        DEG_POWER = 0.5
        src, dst = (edge_index[0], edge_index[1])
        n = x.shape[0]
        deg = jnp.maximum(jnp.zeros((n,), x.dtype).at[dst].add(1.0), 1.0)
        edge_weight = (deg[src] * deg[dst]) ** (-DEG_POWER)
        edge_msg = jax.nn.relu(edge_attr @ W1e + b1e) @ W2e + b2e
        messages = (x[src] + edge_msg) * edge_weight[:, None]
        agg = jax.ops.segment_sum(messages, dst, num_segments=n)
        combined = (1.0 + gin_eps) * x + agg
        h = jax.nn.relu(combined @ W1n + b1n) @ W2n + b2n
        out = h + x
        out = out * jax.lax.rsqrt(jnp.mean(out * out, axis=-1, keepdims=True) + RMS_EPS) * rms_w
        return out
    edge_index = jnp.stack([src, dst])
    h = jnp.maximum(_layernorm(x, axis=-1), 0.0)
    x = x + _L0_gnn_ref(h, edge_index, edge_attr_64, L0_gnn_W1n, L0_gnn_b1n, L0_gnn_W2n, L0_gnn_b2n, L0_gnn_W1e, L0_gnn_b1e, L0_gnn_W2e, L0_gnn_b2e, L0_gnn_gin_eps, L0_gnn_rms_w)
    return x

_drawn_inputs = setup_inputs


def setup_inputs(seed=0):
    import zlib

    import numpy as np

    out = dict(_drawn_inputs(seed))
    spreads = {'L0_gnn_b1n': (0.0, 1.396),
     'L0_gnn_b2n': (0.0, 0.606),
     'L0_gnn_b1e': (0.0, 2.0),
     'L0_gnn_b2e': (0.0, 2.0),
     'L0_gnn_rms_w': (1.0, 0.2)}
    factors = {'edge_attr_64': 8.0, 'L0_gnn_W1e': 8.0, 'L0_gnn_W2e': 3.995}
    for name, (base, spread) in spreads.items():
        noise = np.random.default_rng([zlib.crc32(name.encode()), seed]).standard_normal(out[name].shape)
        drawn = base * np.exp(spread * noise) if base else spread * noise
        out[name] = jnp.asarray(drawn.astype(out[name].dtype))
    for name, factor in factors.items():
        out[name] = (out[name] * factor).astype(out[name].dtype)
    return out
```

```python
import concourse.bass as bass
from concourse import mybir
from contextlib import ExitStack

F32 = mybir.dt.float32
BF16 = mybir.dt.bfloat16
I32 = mybir.dt.int32
ALU = mybir.AluOpType
ACT = mybir.ActivationFunctionType
AX = mybir.AxisListType

N, E, D, ED = 6250, 206250, 128, 64
NB = 125
NBLK = N // NB
T = 16
GT = 8
GP = GT // 2
NG = T // GT
CH = 128 * T
NC = -(-E // CH)
LAST = NC - 1
TAIL0 = E - CH
TWICE = LAST * CH - TAIL0
WIN = 128
NWIN = -(-N // WIN)
ROW = 1 + D
XW = ROW + D
MASKED = -4096.0
EPS_LN = 1e-5
EPS_RMS = 1.1920929e-07


def build(nc, t):
    ctx = ExitStack()
    with ctx:
        def sb(name, shape, dt=F32):
            return ctx.enter_context(nc.sbuf_tensor(name, shape, dt))

        def sem(name, scope=ctx):
            return scope.enter_context(nc.semaphore(name))

        table = nc.dram_tensor("node_rows", (N, ROW), F32).ap()

        x_sb = sb("x_sb", [NB, NBLK, D])
        h_sb = sb("h_sb", [NB, NBLK, D])
        acc = sb("acc", [128, N + WIN])
        edge_rows = sb("edge_rows", [128, 2, T, XW])
        s_nd = sb("s_nd", [NB, NBLK])
        dst_f = sb("dst_f", [128, NC, T])
        rel = sb("rel", [128, NC, T])
        base_b = sb("base_b", [128, NC])
        base_i = sb("base_i", [1, NC], I32)
        npass_i = sb("npass_i", [1, 1], I32)
        w1e = sb("w1e", [2 * ED, D])
        b1_row = sb("b1_row", [1, 2, GP * D])
        b1_part = sb("b1_part", [1, 3, GP * D], BF16)
        b1_split = sb("b1_split", [3, GP * D], BF16)
        ones_bf = sb("ones_bf", [3, 128], BF16)
        w2e = sb("w2e", [D, D])
        w1n = sb("w1n", [D, D])
        w2n = sb("w2n", [D, D])
        b1n = sb("b1n", [D, 1])
        b2e_b = sb("b2e_b", [128, D])
        b2n_b = sb("b2n_b", [128, D])
        rmsw_b = sb("rmsw_b", [128, D])
        eps1 = sb("eps1", [128, 1])
        ident = sb("ident", [128, 128])
        iota = sb("iota", [128, WIN])
        ones = sb("ones", [128, 128])
        stat = sb("stat", [128, 4, NBLK])
        a_sb = sb("a_sb", [128, 2, T, ED])
        idx = sb("idx", [128, 2, T], I32)
        aT = sb("aT", [2 * ED, 2, GP, 128])
        onehot = sb("onehot", [128, 2, GT, WIN])
        win_sb = sb("win_sb", [128, 2 * D])
        rT_sb = sb("rT_sb", [128, WIN])
        bank = [ctx.enter_context(nc.psum_tensor(f"bank{i}", [128, 512], F32)) for i in range(8)]

        w_a = acc[:, 0:NC * T].rearrange("p (c t) -> p c t", t=T)
        w_b = acc[:, NC * T:2 * NC * T].rearrange("p (c t) -> p c t", t=T)
        o = 2 * NC * T
        w_i = acc[:, o:o + NC * T].bitcast(I32).rearrange("p (c t) -> p c t", t=T)
        oh_lo = acc[:, o:o + T * NB].bitcast(BF16).rearrange("p (u t n) -> p u t n", u=2, t=T)
        oh_hi = acc[:, o + T * NB:o + T * NB + T * NBLK].bitcast(BF16).rearrange("p (u t n) -> p u t n", u=2, t=T)
        lo_bf = sb("lo_bf", [128, NC, T], BF16)
        hi_bf = sb("hi_bf", [128, NC, T], BF16)
        iota_lo = sb("iota_lo", [128, NB], BF16)
        flat_rows = edge_rows[:, :, :, :].rearrange("p u t w -> p (u t w)")
        rows_out = flat_rows[0:NB, 0:NBLK * ROW].rearrange("p (k w) -> p k w", w=ROW)
        square = flat_rows[0:NB, 0:NBLK * D].rearrange("p (k w) -> p k w", w=D)

        with ExitStack() as st:
            x_in = sem("x_in", st)
            dst_in = sem("dst_in", st)
            w_in = sem("w_in", st)
            consts = sem("consts", st)
            dve = sem("dve_step", st)
            centred = sem("centred", st)
            squared = sem("squared", st)
            var_ready = sem("var_ready", st)
            std_ready = sem("std_ready", st)
            scaled = sem("scaled", st)
            h_ready = sem("h_ready", st)
            base_row = sem("base_row", st)
            base_bc = sem("base_bc", st)
            dst_masked = sem("dst_masked", st)
            split_ready = sem("split_ready", st)
            lo_ready = sem("lo_ready", st)
            hi_ready = sem("hi_ready", st)
            oh_used = sem("oh_used", st)
            deg_ready = sem("deg_ready", st)
            root_ready = sem("root_ready", st)
            viol_ready = sem("viol_ready", st)
            viol_sum = sem("viol_sum", st)
            rows_ready = sem("rows_ready", st)
            rows_stored = sem("rows_stored", st)
            b1_parts = sem("b1_parts", st)
            b1_in = sem("b1_in", st)
            block = st.enter_context(nc.Block())

            @block.sync
            def _(sp):
                sp.dma_start(dst_f[:, 0:LAST, :].bitcast(I32), t["dst"][0:LAST * CH].rearrange("(c p t) -> p c t", p=128, t=T)).then_inc(dst_in, 16)
                sp.dma_start(dst_f[:, LAST, :].bitcast(I32), t["dst"][TAIL0:E].rearrange("(p t) -> p t", t=T)).then_inc(dst_in, 16)
                for i, (to, of) in enumerate([
                    (w1e[0:ED, :], t["W1e"]), (w1e[ED:2 * ED, :], t["W1e"]), (w2e[:, :], t["W2e"]),
                    (w1n[:, :], t["W1n"]), (w2n[:, :], t["W2n"]), (b1n[:, :], t["b1n"].rearrange("o d -> d o")),
                    (b2e_b[:, :], t["b2e"].broadcast_to((128, D))), (b2n_b[:, :], t["b2n"].broadcast_to((128, D))),
                    (rmsw_b[:, :], t["rms_w"].broadcast_to((128, D))), (eps1[:, :], t["eps"].broadcast_to((128, 1))),
                    (b1_row[0:1, 0, :].rearrange("o (g d) -> o g d", d=D), t["b1e"].unsqueeze(1).broadcast_to((1, GP, D))),
                ]):
                    sp.dma_start(to, of).then_inc(w_in, 16)
                sp.wait_ge(b1_parts, 1)
                sp.dma_start(b1_split[:, :], b1_part[:, :, :]).then_inc(b1_in, 16)
                sp.wait_ge(b1_in, 16)
                sp.wait_ge(rows_ready, 2)
                sp.dma_start(table.rearrange("(k p) w -> p k w", p=NB), rows_out).then_inc(rows_stored, 16)
                sp.wait_ge(rows_stored, 16)

            @block.scalar
            def _(act):
                act.dma_start(x_sb[:, :, :], t["x"].rearrange("(k p) d -> p k d", p=NB)).then_inc(x_in, 16)
                act.wait_ge(centred, 1)
                nc.scalar.activation(square, h_sb[:, :, :], ACT.Square).then_inc(squared, 1)
                act.wait_ge(var_ready, 1)
                nc.scalar.activation(stat[0:NB, 1, :], stat[0:NB, 0, :], ACT.Sqrt).then_inc(std_ready, 1)
                act.wait_ge(scaled, 1)
                nc.scalar.activation(h_sb[:, :, :], h_sb[:, :, :], ACT.Relu).then_inc(h_ready, 1)
                act.wait_ge(deg_ready, 2)
                nc.scalar.activation(stat[0:NB, 3, :], stat[0:NB, 2, :], ACT.Sqrt).then_inc(root_ready, 1)

            @block.gpsimd
            def _(pool):
                nc.gpsimd.memset(ones[:, :], 1.0).then_inc(consts, 1)
                nc.gpsimd.iota(iota[:, :], pattern=[[1, WIN]], base=0, channel_multiplier=0,
                               allow_small_or_imprecise_dtypes=True).then_inc(consts, 1)
                nc.gpsimd.iota(iota_lo[:, :], pattern=[[1, NB]], base=0, channel_multiplier=0,
                               allow_small_or_imprecise_dtypes=True).then_inc(consts, 1)
                pool.wait_ge(consts, 3)
                nc.gpsimd.affine_select(out=ident[:, :], in_=ones[:, :], compare_op=ALU.is_equal, fill=0.0, base=0,
                                        pattern=[[-1, 128]], channel_multiplier=1).then_inc(consts, 1)
                pool.wait_ge(base_row, 1)
                nc.gpsimd.affine_select(out=dst_f[:, LAST, :], in_=dst_f[:, LAST, :], compare_op=ALU.is_ge,
                                        fill=MASKED, base=-TWICE, pattern=[[1, T]],
                                        channel_multiplier=T).then_inc(dst_masked, 1)

            @block.tensor
            def _(pe):
                pe.wait_ge(consts, 4)
                pe.wait_ge(base_row, 1)
                nc.tensor.matmul(bank[1][:, 0:NC], ones[0:1, :], base_b[0:1, :], start=True, stop=True).then_inc(base_bc, 1)

                def chunk(c, u, first, last):
                    pe.wait_ge(lo_ready, c + 1)
                    pe.wait_ge(hi_ready, c + 1)
                    for j in range(T):
                        mm = nc.tensor.matmul(bank[0][0:NB, 0:NBLK], oh_lo[:, u, j, :], oh_hi[:, u, j, :],
                                              start=first and j == 0, stop=last and j == T - 1, skip_group_check=True)
                    mm.then_inc(oh_used, 1)
                chunk(0, 0, True, False)
                chunk(1, 1, False, False)
                with pe.Fori(1, LAST // 2) as i:
                    for u in range(2):
                        chunk(2 * i + u, u, False, False)
                chunk(LAST, 0, False, True)
                pe.wait_ge(viol_ready, 1)
                nc.tensor.matmul(bank[2][:, 0:1], ones[:, :], stat[:, 3, 0:1], start=True, stop=True).then_inc(viol_sum, 1)

            @block.vector
            def _(v):
                n = [0]

                def step(ins):
                    n[0] += 1
                    ins.then_inc(dve, 1)
                    v.wait_ge(dve, n[0])

                def bc(ap):
                    return ap.unsqueeze(2).broadcast_to((NB, NBLK, D))

                nc.vector.memset(ones_bf[:, :], 1.0)
                v.wait_ge(dst_in, 32)
                step(nc.vector.tensor_copy(w_a, dst_f[:, :, :].bitcast(I32)))
                step(nc.vector.tensor_copy(dst_f[:, :, :], w_a))
                nc.vector.tensor_copy(base_b[0:1, :], dst_f[0:1, :, 0]).then_inc(base_row, 1)
                v.wait_ge(dst_masked, 1)
                v.wait_ge(base_bc, 1)
                step(nc.vector.tensor_copy(base_b[:, :], bank[1][:, 0:NC]))
                step(nc.vector.tensor_tensor(rel[:, :, :], dst_f[:, :, :],
                                             base_b[:, :].unsqueeze(2).broadcast_to((128, NC, T)), ALU.subtract))
                step(nc.vector.tensor_scalar(w_a, rel[:, :, :], 0.0, None, ALU.is_lt))
                step(nc.vector.scalar_tensor_tensor(out=w_a, in0=dst_f[:, :, :], scalar=0.0, in1=w_a,
                                                    op0=ALU.is_ge, op1=ALU.mult))
                step(nc.vector.scalar_tensor_tensor(out=w_a, in0=rel[:, :, :], scalar=float(WIN), in1=w_a,
                                                    op0=ALU.is_ge, op1=ALU.add))
                step(nc.vector.reduce_sum(stat[:, 3, 0:1], w_a.rearrange("p c t -> p (c t)"), AX.X))
                nc.vector.tensor_scalar(w_i, dst_f[:, :, :], 1.0 / NB, None, ALU.mult).then_inc(viol_ready, 1)
                v.wait_ge(viol_ready, 1)
                step(nc.vector.tensor_copy(w_a, w_i))
                step(nc.vector.scalar_tensor_tensor(out=w_a, in0=w_a, scalar=float(-NB), in1=dst_f[:, :, :],
                                                    op0=ALU.mult, op1=ALU.add))
                step(nc.vector.tensor_scalar(w_b, w_a, 0.0, float(NB), ALU.is_lt, ALU.mult))
                step(nc.vector.tensor_tensor(w_a, w_a, w_b, ALU.add))
                step(nc.vector.tensor_scalar(w_b, w_a, float(NB), float(-NB), ALU.is_ge, ALU.mult))
                step(nc.vector.tensor_tensor(w_a, w_a, w_b, ALU.add))
                step(nc.vector.tensor_copy(lo_bf[:, :, :], w_a))
                step(nc.vector.tensor_tensor(w_b, dst_f[:, :, :], w_a, ALU.subtract))
                nc.vector.tensor_scalar(hi_bf[:, :, :], w_b, 1.0 / NB, None, ALU.mult).then_inc(split_ready, 1)

                def chunk(c, u, free):
                    if free is not None:
                        v.wait_ge(oh_used, free)
                    nc.vector.tensor_tensor(oh_hi[:, u, :, :],
                                            hi_bf[:, bass.ds(c, 1), :].rearrange("p o t -> p (o t)").unsqueeze(2).broadcast_to((128, T, NBLK)),
                                            iota_lo[:, 0:NBLK].unsqueeze(1).broadcast_to((128, T, NBLK)),
                                            ALU.is_equal).then_inc(hi_ready, 1)
                    nc.vector.tensor_tensor(oh_lo[:, u, :, :],
                                            lo_bf[:, bass.ds(c, 1), :].rearrange("p o t -> p (o t)").unsqueeze(2).broadcast_to((128, T, NB)),
                                            iota_lo[:, :].unsqueeze(1).broadcast_to((128, T, NB)),
                                            ALU.is_equal).then_inc(lo_ready, 1)
                v.wait_ge(consts, 4)
                v.wait_ge(split_ready, 1)
                chunk(0, 0, None)
                chunk(1, 1, None)
                with v.Fori(1, LAST // 2) as i:
                    for u in range(2):
                        chunk(2 * i + u, u, 2 * i + u - 1)
                chunk(LAST, 0, LAST - 1)

                v.wait_ge(x_in, 16)
                step(nc.vector.reduce_sum(stat[0:NB, 0, :], x_sb[:, :, :], AX.X))
                step(nc.vector.tensor_scalar(stat[0:NB, 0, :], stat[0:NB, 0, :], -1.0 / D, None, ALU.mult))
                nc.vector.tensor_tensor(h_sb[:, :, :], x_sb[:, :, :], bc(stat[0:NB, 0, :]), ALU.add).then_inc(centred, 1)
                v.wait_ge(squared, 1)
                step(nc.vector.reduce_sum(stat[0:NB, 0, :], square, AX.X))
                nc.vector.tensor_scalar(stat[0:NB, 0, :], stat[0:NB, 0, :], 1.0 / D, EPS_LN, ALU.mult, ALU.add).then_inc(var_ready, 1)
                v.wait_ge(std_ready, 1)
                step(nc.vector.reciprocal(stat[0:NB, 1, :], stat[0:NB, 1, :]))
                nc.vector.tensor_tensor(h_sb[:, :, :], h_sb[:, :, :], bc(stat[0:NB, 1, :]), ALU.mult).then_inc(scaled, 1)

                v.wait_ge(viol_sum, 1)
                step(nc.vector.tensor_scalar(stat[:, 0, 0:1], bank[2][:, 0:1], 0.0, None, ALU.is_equal))
                step(nc.vector.tensor_scalar(base_b[:, :], base_b[:, :], stat[:, 0, 0:1], None, ALU.mult))
                step(nc.vector.tensor_scalar(npass_i[:, :], stat[0:1, 0, 0:1], float(1 - NWIN), float(NWIN), ALU.mult, ALU.add))

                v.wait_ge(oh_used, NC)
                nc.vector.tensor_scalar(stat[0:NB, 2, :], bank[0][0:NB, 0:NBLK], 1.0, None, ALU.max).then_inc(deg_ready, 2)
                v.wait_ge(root_ready, 1)
                step(nc.vector.reciprocal(s_nd[:, :], stat[0:NB, 3, :]))
                nc.vector.tensor_copy(rows_out[:, :, 0:1], s_nd[:, :].unsqueeze(2)).then_inc(rows_ready, 1)
                v.wait_ge(h_ready, 1)
                v.wait_ge(w_in, 176)
                nc.vector.tensor_tensor(rows_out[:, :, 1:ROW], h_sb[:, :, :],
                                        b2e_b[0:NB, :].unsqueeze(1).broadcast_to((NB, NBLK, D)), ALU.add).then_inc(rows_ready, 1)
                step(nc.vector.tensor_copy(b1_part[:, 0, :], b1_row[:, 0, :]))
                step(nc.vector.tensor_tensor(b1_row[:, 1, :], b1_row[:, 0, :], b1_part[:, 0, :], ALU.subtract))
                step(nc.vector.tensor_copy(b1_part[:, 1, :], b1_row[:, 1, :]))
                step(nc.vector.tensor_tensor(b1_row[:, 0, :], b1_row[:, 1, :], b1_part[:, 1, :], ALU.subtract))
                nc.vector.tensor_copy(b1_part[:, 2, :], b1_row[:, 0, :]).then_inc(b1_parts, 1)
                step(nc.vector.memset(acc[:, :], 0.0))
                step(nc.vector.tensor_scalar(eps1[:, :], eps1[:, :], 1.0, None, ALU.add))

        n_pass = nc.values_load(npass_i[0:1, 0:1], min_val=1, max_val=NWIN)
        with nc.Fori(0, n_pass) as _:
            edge_pass(nc, t, table, dst_f, rel, base_b, base_i, a_sb, idx, aT, edge_rows, onehot, iota, w1e, b1_split, ones_bf, w2e,
                      ident, win_sb, rT_sb, acc, bank)

        with ExitStack() as st:
            staged = sem("staged", st)
            turned = sem("turned", st)
            comb_part = sem("comb_part", st)
            combined = sem("combined", st)
            combT_ps = sem("combT_ps", st)
            combT_ready = sem("combT_ready", st)
            hidden_ps = sem("hidden_ps", st)
            hidden_ready = sem("hidden_ready", st)
            mlp_ps = sem("mlp_ps", st)
            out_part = sem("out_part", st)
            out_ready = sem("out_ready", st)
            sums_ready = sem("sums_ready", st)
            ms_ready = sem("ms_ready", st)
            rms_ready = sem("rms_ready", st)
            dve = sem("dve_step3", st)
            y_ready = sem("y_ready", st)
            stored = sem("stored", st)
            block = st.enter_context(nc.Block())
            G = 2
            STEPS = NBLK // G
            o = [0]

            def scratch(rows, *dims):
                size = 1
                for d in dims:
                    size *= d
                ap = flat_rows[0:rows, o[0]:o[0] + size]
                o[0] += size
                return ap.rearrange("p (a b) -> p a b", b=dims[-1]) if len(dims) > 1 else ap

            stage = scratch(128, G, NB)
            comb = scratch(NB, G, D)
            combT = scratch(128, G * NB)
            hidT = scratch(128, G, NB)
            junk = scratch(NB, G, D)
            agg_n = bank[0][0:NB, 0:G * D].rearrange("p (g d) -> p g d", d=D)
            combT_b = bank[1][:, 0:G * NB].rearrange("p (g n) -> p g n", n=NB)
            hidden_b = bank[2][:, 0:G * NB]
            mlp_b = bank[3][0:NB, 0:G * D].rearrange("p (g d) -> p g d", d=D)

            @block.scalar
            def _(act):
                def one(i, later):
                    if later:
                        act.wait_ge(turned, i)
                    nc.scalar.activation(stage.rearrange("p g n -> p (g n)"), acc[:, bass.ds(i * (G * NB), G * NB)],
                                         ACT.Copy).then_inc(staged, 1)
                    act.wait_ge(combT_ps, i + 1)
                    nc.scalar.activation(combT, combT_b.rearrange("p g n -> p (g n)"), ACT.Copy).then_inc(combT_ready, 1)
                    act.wait_ge(hidden_ps, i + 1)
                    nc.scalar.activation(hidT.rearrange("p g n -> p (g n)"), hidden_b, ACT.Relu,
                                         bias=b1n[:, 0:1]).then_inc(hidden_ready, 1)
                    act.wait_ge(out_ready, i + 1)
                    for g in range(G):
                        nc.scalar.activation(junk[:, g, :], h_sb[:, bass.ds(i * G + g, 1), :].rearrange("p o d -> p (o d)"),
                                             ACT.Square, accum_out=stat[0:NB, 0, bass.ds(i * G + g, 1)]).then_inc(sums_ready, 1)
                one(0, False)
                with act.Fori(1, STEPS) as i:
                    one(i, True)
                act.wait_ge(ms_ready, 1)
                nc.scalar.activation(stat[0:NB, 1, :], stat[0:NB, 0, :], ACT.Sqrt).then_inc(rms_ready, 1)

            @block.tensor
            def _(pe):
                def one(i):
                    pe.wait_ge(staged, i + 1)
                    for g in range(G):
                        mm = nc.tensor.transpose(agg_n[:, g, :], stage[:, g, :], ident[:, :])
                    mm.then_inc(turned, 1)
                    pe.wait_ge(combined, i + 1)
                    for g in range(G):
                        mm = nc.tensor.transpose(combT_b[:, g, :], comb[:, g, :], ident[0:NB, 0:NB])
                    mm.then_inc(combT_ps, 1)
                    pe.wait_ge(combT_ready, i + 1)
                    nc.tensor.matmul(hidden_b, w1n[:, :], combT, start=True, stop=True).then_inc(hidden_ps, 1)
                    pe.wait_ge(hidden_ready, i + 1)
                    for g in range(G):
                        mm = nc.tensor.matmul(mlp_b[:, g, :], hidT[:, g, :], w2n[:, :], start=True, stop=True)
                    mm.then_inc(mlp_ps, 1)
                with pe.Fori(0, STEPS) as i:
                    one(i)

            @block.vector
            def _(v):
                def one(i):
                    hs = h_sb[:, bass.ds(i * G, G), :]
                    v.wait_ge(turned, i + 1)
                    for g in range(G):
                        nc.vector.tensor_scalar(comb[:, g, :], agg_n[:, g, :], s_nd[:, bass.ds(i * G + g, 1)], None,
                                                ALU.mult).then_inc(comb_part, 1)
                    v.wait_ge(comb_part, G * i + G)
                    nc.vector.scalar_tensor_tensor(out=comb, in0=hs, scalar=eps1[0:NB, 0:1], in1=comb,
                                                   op0=ALU.mult, op1=ALU.add).then_inc(combined, 1)
                    v.wait_ge(mlp_ps, i + 1)
                    nc.vector.tensor_tensor(hs, mlp_b, hs, ALU.add).then_inc(out_part, 1)
                    v.wait_ge(out_part, i + 1)
                    nc.vector.tensor_tensor(hs, hs, b2n_b[0:NB, :].unsqueeze(1).broadcast_to((NB, G, D)),
                                            ALU.add).then_inc(out_ready, 1)
                with v.Fori(0, STEPS) as i:
                    one(i)
                n = [0]

                def step(ins):
                    n[0] += 1
                    ins.then_inc(dve, 1)
                    v.wait_ge(dve, n[0])

                v.wait_ge(sums_ready, G * STEPS)
                nc.vector.tensor_scalar(stat[0:NB, 0, :], stat[0:NB, 0, :], 1.0 / D, EPS_RMS, ALU.mult, ALU.add).then_inc(ms_ready, 1)
                v.wait_ge(rms_ready, 1)
                step(nc.vector.reciprocal(stat[0:NB, 1, :], stat[0:NB, 1, :]))
                for part in range(2):
                    k = slice(part * NBLK // 2, (part + 1) * NBLK // 2)
                    shape = (NB, NBLK // 2, D)
                    step(nc.vector.tensor_tensor(h_sb[:, k, :], h_sb[:, k, :], stat[0:NB, 1, k].unsqueeze(2).broadcast_to(shape), ALU.mult))
                    step(nc.vector.tensor_tensor(h_sb[:, k, :], h_sb[:, k, :], rmsw_b[0:NB, :].unsqueeze(1).broadcast_to(shape), ALU.mult))
                    nc.vector.tensor_tensor(h_sb[:, k, :], h_sb[:, k, :], x_sb[:, k, :], ALU.add).then_inc(y_ready, 1)

            @block.sync
            def _(sp):
                for part in range(2):
                    k = slice(part * NBLK // 2, (part + 1) * NBLK // 2)
                    rows = slice(k.start * NB, k.stop * NB)
                    sp.wait_ge(y_ready, part + 1)
                    sp.dma_start(t["out"][rows, :].rearrange("(k p) d -> p k d", p=NB), h_sb[:, k, :]).then_inc(stored, 16)
                sp.wait_ge(stored, 32)


def edge_pass(nc, t, table, dst_f, rel, base_b, base_i, a_sb, idx, aT, edge_rows, onehot, iota, w1e, b1_split, ones_bf, w2e,
              ident, win_sb, rT_sb, acc, bank):
    with ExitStack() as st:
        def sem(name):
            return st.enter_context(nc.semaphore(name))

        rel_ready = sem("rel_ready")
        a_in = [sem(f"a_in{u}") for u in range(2)]
        idx_in = [sem(f"idx_in{u}") for u in range(2)]
        gathered = [sem(f"gathered{u}") for u in range(2)]
        slot_free = sem("slot_free")
        aT_ps = sem("aT_ps")
        aT_ready = sem("aT_ready")
        z_ps = sem("z_ps")
        r_ready = sem("r_ready")
        onehot_ready = sem("onehot_ready")
        summed = sem("summed")
        win_ready = sem("win_ready")
        rT_ps = sem("rT_ps")
        rT_ready = sem("rT_ready")
        win_ps = sem("win_ps")
        added = sem("added")
        every = [rel_ready, *a_in, *idx_in, *gathered, slot_free, aT_ps, aT_ready, z_ps, r_ready, onehot_ready, summed,
                 win_ready, rT_ps, rT_ready, win_ps, added]
        aT_bank = bank[0:2]
        z_bank = bank[2:4]
        sum_bank = [bank[4][:, 0:2 * D], bank[5][:, 0:2 * D]]
        rT_bank, win_bank = bank[6][:, 0:WIN], bank[7][:, 0:WIN]

        def chunks(eng, one):
            one(0, 0, 0)
            one(1, 1, 1)
            with eng.Fori(1, LAST // 2) as i:
                for u in range(2):
                    one(2 * i + u, u, 2)
            one(LAST, 0, 2)

        with nc.Block() as block:
            @block.sync
            def _(sp):
                def one(c, u, past):
                    start = TAIL0 if c is LAST else c * CH
                    if past == 2:
                        sp.wait_ge(gathered[u], (c - u) * (8 * T))
                    sp.dma_start(idx[:, u, :], t["src"][bass.ds(start, CH)].rearrange("(p t) -> p t", t=T)).then_inc(idx_in[u], 16)
                    if past == 2:
                        sp.wait_ge(aT_ps, (c - 1) * NG)
                    sp.dma_start(a_sb[:, u, :, :], t["attr"][bass.ds(start, CH), :].rearrange("(p t) d -> p t d", t=T)).then_inc(a_in[u], 16)
                chunks(sp, one)

            @block.gpsimd
            def _(pool):
                def one(c, u, past):
                    pool.wait_ge(idx_in[u], (c - u) * 8 + 16)
                    if past == 2:
                        pool.wait_ge(summed, (c - 1) * NG)
                        pool.sem_inc(slot_free, 1)
                    for j in range(T):
                        nc.gpsimd.indirect_dma_start(
                            out=edge_rows[:, u, j, 0:ROW], out_offset=None, in_=table,
                            in_offset=bass.IndirectOffsetOnAxis(ap=idx[:, u, j:j + 1], axis=0)).then_inc(gathered[u], 16)
                chunks(pool, one)
                pool.wait_ge(gathered[0], (LAST // 2 + 1) * T * 16)
                pool.wait_ge(gathered[1], (LAST // 2) * T * 16)

            @block.tensor
            def _(pe):
                def edge_mlp(q, slot, first):
                    pe.wait_ge(aT_ready, q + 1)
                    if not first:
                        pe.wait_ge(r_ready, q)
                    for odd in range(2):
                        nc.tensor.matmul(z_bank[odd][:, :], ones_bf[:, :], b1_split[:, :], start=True, stop=False)
                    for j in range(GP):
                        for odd in range(2):
                            half = slice(odd * ED, odd * ED + ED)
                            mm = nc.tensor.matmul(z_bank[odd][:, j * D:(j + 1) * D], aT[half, slot, j, :],
                                                  w1e[half, :], start=False, stop=j == GP - 1)
                    mm.then_inc(z_ps, 1)

                def sum_group(c, u, g, first):
                    q = c * NG + g
                    pe.wait_ge(onehot_ready, q + 1)
                    pe.wait_ge(r_ready, q + 1)
                    if g == 0 and not first:
                        pe.wait_ge(win_ready, c - 1)
                    for j in range(GT):
                        k = g * GT + j
                        mm = nc.tensor.matmul(sum_bank[u], onehot[:, g % 2, j, :], edge_rows[:, u, k, 1:XW],
                                              start=k == 0, stop=k == T - 1)
                    mm.then_inc(summed, 1)

                def turn_relu(c):
                    pe.wait_ge(win_ready, c + 1)
                    nc.tensor.transpose(rT_bank, win_sb[:, D:2 * D], ident[:, :]).then_inc(rT_ps, 1)

                def window(c, first):
                    pe.wait_ge(rT_ready, c + 1)
                    if not first:
                        pe.wait_ge(added, c)
                    nc.tensor.matmul(win_bank, w2e[:, :], rT_sb[:, :], start=True, stop=False)
                    nc.tensor.matmul(win_bank, win_sb[:, 0:D], ident[:, :], start=False, stop=True).then_inc(win_ps, 1)

                def one(c, u, past):
                    for g in range(NG):
                        q = c * NG + g
                        if g == 0:
                            pe.wait_ge(a_in[u], (c - u) * 8 + 16)
                        if not (past == 0 and g < 2):
                            pe.wait_ge(aT_ready, q - 1)
                        for j in range(GP):
                            k = g * GT + 2 * j
                            mm = nc.tensor.transpose(aT_bank[g % 2][:, j * 128:(j + 1) * 128],
                                                     a_sb[:, u, k:k + 2, :].rearrange("p j d -> p (j d)"), ident[:, :])
                        mm.then_inc(aT_ps, 1)
                        if not (past == 0 and g == 0):
                            edge_mlp(q - 1, (g + 1) % 2, past == 0)
                        if past >= 1:
                            sum_group(c - 1, 1 - u, g, past < 2)
                        if past == 2 and g == 0:
                            turn_relu(c - 2)
                        if past == 2 and g == 1:
                            window(c - 2, False)
                one(0, 0, 0)
                one(1, 1, 1)
                with pe.Fori(1, LAST // 2) as i:
                    for u in range(2):
                        one(2 * i + u, u, 2)
                one(LAST, 0, 2)
                edge_mlp(NC * NG - 1, 1, False)
                for g in range(NG):
                    sum_group(LAST, 0, g, False)
                    if g == 0:
                        turn_relu(LAST - 1)
                window(LAST - 1, False)
                turn_relu(LAST)
                window(LAST, False)

            @block.scalar
            def _(act):
                def relu(c, u, g, free):
                    act.wait_ge(z_ps, c * NG + g + 1)
                    if g == 0 and free:
                        act.wait_ge(summed, (c - 1) * NG)
                    for odd in range(2):
                        ins = nc.scalar.activation(
                            edge_rows[:, u, g * GT + odd:(g + 1) * GT:2, ROW:XW],
                            z_bank[odd][:, :].rearrange("p (j d) -> p j d", d=D), ACT.Relu)
                    ins.then_inc(r_ready, 1)

                def one(c, u, past):
                    for g in range(NG):
                        q = c * NG + g
                        act.wait_ge(aT_ps, q + 1)
                        if not (past == 0 and g < 2):
                            act.wait_ge(z_ps, q - 1)
                        nc.scalar.activation(aT[:, g % 2, :, :],
                                             aT_bank[g % 2][:, :].rearrange("p (j n) -> p j n", n=128),
                                             ACT.Copy).then_inc(aT_ready, 1)
                        if g > 0:
                            relu(c, u, g - 1, past == 2)
                        elif past >= 1:
                            relu(c - 1, 1 - u, NG - 1, False)
                chunks(act, one)
                relu(LAST, 0, NG - 1, False)

            @block.vector
            def _(v):
                def read_sums(c, u):
                    v.wait_ge(summed, (c + 1) * NG)
                    nc.vector.tensor_copy(win_sb[:, :], sum_bank[u]).then_inc(win_ready, 1)

                def read_rT(c):
                    v.wait_ge(rT_ps, c + 1)
                    nc.vector.tensor_copy(rT_sb[:, :], rT_bank).then_inc(rT_ready, 1)

                def add_window(c, first):
                    base = v.value_load(base_i[0:1, c:c + 1] if isinstance(c, int) else base_i[0:1, bass.ds(c, 1)],
                                        min_val=0, max_val=N - 1)
                    v.wait_ge(win_ps, c + 1)
                    if not first:
                        v.wait_ge(added, c)
                    nc.vector.tensor_tensor(acc[:, bass.ds(base, WIN)], acc[:, bass.ds(base, WIN)], win_bank,
                                            ALU.add).then_inc(added, 1)

                nc.vector.tensor_tensor(rel[:, :, :], dst_f[:, :, :], base_b[:, :].unsqueeze(2).broadcast_to((128, NC, T)),
                                        ALU.subtract).then_inc(rel_ready, 1)
                nc.vector.tensor_copy(base_i[:, :], base_b[0:1, :]).then_inc(rel_ready, 1)
                v.wait_ge(rel_ready, 2)

                def one(c, u, past):
                    if past == 2:
                        add_window(c - 2, False)
                    v.wait_ge(gathered[u], (c - u) * (8 * T) + 16 * T)
                    for g in range(NG):
                        q = c * NG + g
                        if not (past == 0 and g < 2):
                            v.wait_ge(summed, q - 1)
                        for j in range(GT):
                            k = g * GT + j
                            s_edge = edge_rows[:, u, k, 0:1]
                            ins = nc.vector.tensor_scalar(onehot[:, g % 2, j, :], iota[:, :],
                                                          rel[:, bass.ds(c, 1), k], s_edge, ALU.is_equal, ALU.mult)
                        ins.then_inc(onehot_ready, 1)
                        if past >= 1 and g == 0:
                            read_sums(c - 1, 1 - u)
                        if past >= 1 and g == 1:
                            read_rT(c - 1)
                one(0, 0, 0)
                one(1, 1, 1)
                first = [True]
                with v.Fori(1, LAST // 2) as i:
                    for u in range(2):
                        one(2 * i + u, u, 2)
                one(LAST, 0, 2)
                add_window(LAST - 1, False)
                read_sums(LAST, 0)
                read_rT(LAST)
                add_window(LAST, False)
                nc.vector.tensor_scalar(base_b[:, :], base_b[:, :], float(WIN), None, ALU.add)

        nc.all_engine_barrier()
        for s in every:
            nc.sync.sem_clear(s)
        nc.all_engine_barrier()


def kernel(**inputs):
    import numpy as _np
    import concourse.bacc as _bacc
    from concourse import mybir as _mybir
    from concourse.bass_utils import run_bass_kernel_spmd as _run

    nc = _bacc.Bacc("TRN2", target_bir_lowering=False, num_devices=1)
    layout = {
        "x": ("x", (N, D)), "src": ("src", (E,)), "dst": ("dst", (E,)), "attr": ("edge_attr_64", (E, ED)),
        "W1n": ("L0_gnn_W1n", (D, D)), "b1n": ("L0_gnn_b1n", (1, D)), "W2n": ("L0_gnn_W2n", (D, D)),
        "b2n": ("L0_gnn_b2n", (1, D)), "W1e": ("L0_gnn_W1e", (ED, D)), "b1e": ("L0_gnn_b1e", (1, D)),
        "W2e": ("L0_gnn_W2e", (D, D)), "b2e": ("L0_gnn_b2e", (1, D)), "eps": ("L0_gnn_gin_eps", (1, 1)),
        "rms_w": ("L0_gnn_rms_w", (1, D)),
    }
    arrays, t = {}, {}
    for name, (given, shape) in layout.items():
        a = _np.ascontiguousarray(inputs[given]).reshape(shape)
        arrays[f"in_{name}"] = a
        t[name] = nc.dram_tensor(f"in_{name}", shape, _mybir.dt.from_np(a.dtype), kind="ExternalInput").ap()
    t["out"] = nc.dram_tensor("out", (N, D), F32, kind="ExternalOutput").ap()
    build(nc, t)
    r = _run(nc, [arrays], core_ids=[0])
    return r.results[0]["out"]
```

```python
import concourse.bass as bass
from concourse import mybir
from contextlib import ExitStack

F32 = mybir.dt.float32
BF16 = mybir.dt.bfloat16
I32 = mybir.dt.int32
ALU = mybir.AluOpType
ACT = mybir.ActivationFunctionType
AX = mybir.AxisListType

N, E, D, ED = 6250, 206250, 128, 64
NB = 128
NBLK = -(-N // NB)
FULL = N // NB
REST = N - FULL * NB
T = 16
GT = 8
GP = GT // 2
NG = T // GT
CH = 128 * T
NC = -(-E // CH)
LAST = NC - 1
TAIL0 = E - CH
TWICE = LAST * CH - TAIL0
WIN = 128
NWIN = -(-N // WIN)
NCP = NC + NC % 2
LOW = 32
HIGH = WIN // LOW
NH = -(-N // LOW)
QT = T // 4
ROW = 1 + D
XW = ROW + D
ACCW = QT * LOW * NCP // 2
MASKED = -4096.0
EPS_LN = 1e-5
EPS_RMS = 1.1920929e-07


def build(nc, t):
    ctx = ExitStack()
    with ctx:
        def sb(name, shape, dt=F32):
            return ctx.enter_context(nc.sbuf_tensor(name, shape, dt))

        def sem(name, scope=ctx):
            return scope.enter_context(nc.semaphore(name))

        table = nc.dram_tensor("node_rows", (N, ROW), F32).ap()

        x_sb = sb("x_sb", [128, NBLK, D])
        rows = sb("rows", [128, NBLK, ROW])
        acc = sb("acc", [128, ACCW])
        edge_rows = sb("edge_rows", [128, 2, T, XW])
        rel = sb("rel", [128, T, NCP])
        base_f = sb("base_f", [1, NC])
        base_i = sb("base_i", [1, NC], I32)
        npass_i = sb("npass_i", [1, 1], I32)
        npass_f = sb("npass_f", [128, 1])
        fast = sb("fast", [128, 1])
        w1e = sb("w1e", [2 * ED, D])
        w2e = sb("w2e", [D, D])
        w1n = sb("w1n", [D, D])
        w2n = sb("w2n", [D, D])
        b1n = sb("b1n", [D, 1])
        b2e_col = sb("b2e_col", [D, 1])
        b2e_b = sb("b2e_b", [128, D])
        rmsw_b = sb("rmsw_b", [128, D])
        eps1 = sb("eps1", [128, 1])
        bias_split = sb("bias_split", [3, 2, GP * D], BF16)
        ones_bf = sb("ones_bf", [3, 128], BF16)
        zeros_bf = sb("zeros_bf", [1, 512], BF16)
        ident = sb("ident", [128, 128])
        iota = sb("iota", [128, WIN])
        ones = sb("ones", [128, 128])
        stat = sb("stat", [128, 6, NBLK])
        deg = sb("deg", [LOW, NH])
        base_c = sb("base_c", [NC, 1])
        base_all = sb("base_all", [NC, 1])
        base_ci = sb("base_ci", [NC, 1], I32)
        extreme = sb("extreme", [NC, 2])
        outside = sb("outside", [NC, 2])
        where = sb("where", [NC, NH + HIGH - 1])
        where_iota = sb("where_iota", [NC, NH + HIGH - 1])
        fold = sb("fold", [128, LOW])
        win_sb = sb("win_sb", [128, 2 * D])
        rT_sb = sb("rT_sb", [128, WIN])
        bank = [ctx.enter_context(nc.psum_tensor(f"bank{i}", [128, 512], F32)) for i in range(8)]

        work = sb("work", [128, ACCW])
        o = [0]

        def ring(*dims):
            size = 1
            for d in dims:
                size *= d
            o[0] += size
            return work[:, o[0] - size:o[0]]

        a_sb = ring(2, T, ED).rearrange("p (u t d) -> p u t d", u=2, t=T)
        onehot = ring(2, GT, WIN).rearrange("p (u t n) -> p u t n", u=2, t=GT)
        aT = ring(2, GP, 128).rearrange("p (u t n) -> p u t n", u=2, t=GP)
        idx = ring(2, T).bitcast(I32).rearrange("p (u t) -> p u t", u=2)

        dst_i = work[0:NC, 0:CH].bitcast(I32)
        dst_f = work[0:NC, CH:2 * CH]
        rel_c = acc[0:NC, 0:CH]
        parts_f = work[0:1, 2 * CH:2 * CH + 4 * GP * D].rearrange("p (b v d) -> p b v d", b=2, v=2)
        parts = acc[0:1, CH:CH + 3 * GP * D].bitcast(BF16).rearrange("p (b m d) -> p b m d", b=2, m=3)
        low_oh = [r[:, 0:QT * LOW * NCP // 2].bitcast(BF16).rearrange("p (t n c) -> p t n c", t=QT, n=LOW)
                  for r in (acc, work)]
        flat = edge_rows[:, :, :, :].rearrange("p u t w -> p (u t w)")
        o2 = [0]

        def scratch(words):
            o2[0] += words
            return flat[:, o2[0] - words:o2[0]]

        high_oh = scratch(T * HIGH * NCP // 2).bitcast(BF16).rearrange("p (t n c) -> p t n c", t=T, n=HIGH)
        iota_rep = scratch(LOW * NCP // 2).bitcast(BF16).rearrange("p (n c) -> p n c", n=LOW)
        low_bf = scratch(T * NCP // 2).bitcast(BF16).rearrange("p (t c) -> p t c", t=T)
        high_bf = scratch(T * NCP // 2).bitcast(BF16).rearrange("p (t c) -> p t c", t=T)
        rel_i = scratch(T * NCP).bitcast(I32).rearrange("p (t c) -> p t c", t=T)
        counts = low_oh[0].rearrange("p t n c -> p (t n c)").bitcast(F32)[:, 0:HIGH * NC].rearrange("p (h c) -> p h c", h=HIGH)
        counts_c = work[0:NC, 0:HIGH * LOW].rearrange("p (h l) -> p h l", h=HIGH)

        def split_sems(names, scope):
            return [sem(n, scope) for n in names.split()]

        with ExitStack() as st:
            (x_in, dst_in, w_in, bias_in, consts, dve, x_padded, summed_x, mean_ready, summed_sq, rstd_ready,
             std_ready, normed, h_done, found, total_ready, base_ready, base_ps, offset_ready, offset_ps,
             offset_copied, masked, b1n_ps, parts_ready, windows_done) = split_sems(
                "x_in dst_in w_in bias_in consts dve_step x_padded summed_x mean_ready summed_sq rstd_ready "
                "std_ready normed h_done found total_ready base_ready base_ps offset_ready offset_ps "
                "offset_copied masked b1n_ps parts_ready windows_done", st)
            block = st.enter_context(nc.Block())

            @block.sync
            def _(sp):
                sp.dma_start(dst_i[0:LAST, :], t["dst"][0:LAST * CH].rearrange("(c e) -> c e", e=CH)).then_inc(dst_in, 16)
                sp.dma_start(dst_i[LAST:NC, :], t["dst"][TAIL0:E].unsqueeze(0)).then_inc(dst_in, 16)
                for to, of in [
                    (w1e[0:ED, :], t["W1e"]), (w1e[ED:2 * ED, :], t["W1e"]), (w2e[:, :], t["W2e"]),
                    (w1n[:, :], t["W1n"]), (w2n[:, :], t["W2n"]), (b1n[:, :], t["b1n"].rearrange("o d -> d o")),
                    (b2e_col[:, :], t["b2e"].rearrange("o d -> d o")), (b2e_b[:, :], t["b2e"].broadcast_to((128, D))),
                    (rmsw_b[:, :], t["rms_w"].broadcast_to((128, D))), (eps1[:, :], t["eps"].broadcast_to((128, 1))),
                    (parts_f[:, 0, 0, :].rearrange("o (g d) -> o g d", d=D), t["b1e"].unsqueeze(1).broadcast_to((1, GP, D))),
                    (parts_f[:, 1, 0, :].rearrange("o (g d) -> o g d", d=D), t["b2n"].unsqueeze(1).broadcast_to((1, GP, D))),
                ]:
                    sp.dma_start(to, of).then_inc(w_in, 16)
                sp.wait_ge(parts_ready, 1)
                for b in range(2):
                    sp.dma_start(bias_split[:, b, :], parts[:, b, :, :]).then_inc(bias_in, 16)
                sp.wait_ge(bias_in, 32)

            @block.scalar
            def _(act):
                act.wait_ge(x_padded, 1)
                act.dma_start(x_sb[:, 0:FULL, :], t["x"][0:FULL * NB, :].rearrange("(k p) d -> p k d", p=NB)).then_inc(x_in, 16)
                act.dma_start(x_sb[0:REST, FULL, :], t["x"][FULL * NB:N, :]).then_inc(x_in, 16)
                act.wait_ge(x_in, 32)
                for k in range(NBLK):
                    ins = nc.scalar.activation(rows[:, k, 1:ROW], x_sb[:, k, :], ACT.Copy, accum_out=stat[:, 0, k:k + 1])
                ins.then_inc(summed_x, 1)
                act.wait_ge(mean_ready, 1)
                for k in range(NBLK):
                    ins = nc.scalar.activation(rows[:, k, 1:ROW], x_sb[:, k, :], ACT.Square, bias=stat[:, 1, k:k + 1],
                                               accum_out=stat[:, 2, k:k + 1])
                ins.then_inc(summed_sq, 1)
                act.wait_ge(rstd_ready, 1)
                nc.scalar.activation(stat[:, 2, :], stat[:, 2, :], ACT.Sqrt).then_inc(std_ready, 1)
                act.wait_ge(rstd_ready, 2)
                for k in range(NBLK):
                    ins = nc.scalar.activation(rows[:, k, 1:ROW], x_sb[:, k, :], ACT.Relu, bias=stat[:, 4, k:k + 1],
                                               scale=stat[:, 3, k:k + 1])
                ins.then_inc(normed, 1)

            @block.gpsimd
            def _(pool):
                nc.gpsimd.memset(ones[:, :], 1.0).then_inc(consts, 1)
                nc.gpsimd.iota(iota[:, :], pattern=[[1, WIN]], base=0, channel_multiplier=0,
                               allow_small_or_imprecise_dtypes=True).then_inc(consts, 1)
                nc.gpsimd.iota(iota_rep, pattern=[[1, LOW], [0, NCP]], base=0, channel_multiplier=0,
                               allow_small_or_imprecise_dtypes=True).then_inc(consts, 1)
                nc.gpsimd.iota(where_iota[:, :], pattern=[[LOW, NH + HIGH - 1]], base=-LOW * (HIGH - 1),
                               channel_multiplier=0, allow_small_or_imprecise_dtypes=True).then_inc(consts, 1)
                pool.wait_ge(consts, 4)
                nc.gpsimd.affine_select(out=ident[:, :], in_=ones[:, :], compare_op=ALU.is_equal, fill=0.0, base=0,
                                        pattern=[[-1, 128]], channel_multiplier=1).then_inc(consts, 1)
                pool.wait_ge(offset_copied, 1)
                nc.gpsimd.affine_select(out=rel[:, :, LAST], in_=rel[:, :, LAST], compare_op=ALU.is_ge,
                                        fill=MASKED, base=-TWICE, pattern=[[1, T]],
                                        channel_multiplier=T).then_inc(masked, 1)
                pool.wait_ge(normed, 1)
                pool.wait_ge(w_in, 192)
                nc.gpsimd.tensor_tensor(rows[:, :, 1:ROW], rows[:, :, 1:ROW],
                                        b2e_b[:, :].unsqueeze(1).broadcast_to((128, NBLK, D)), ALU.add).then_inc(h_done, 1)

            @block.tensor
            def _(pe):
                pe.wait_ge(consts, 5)
                pe.wait_ge(found, 1)
                for j in range(2):
                    mm = nc.tensor.matmul(bank[4][:, 0:1], ones[0:NC, :], outside[:, j:j + 1], start=j == 0, stop=j == 1)
                mm.then_inc(total_ready, 1)
                pe.wait_ge(base_ready, 1)
                nc.tensor.transpose(bank[5][0:1, 0:NC], base_c[:, :], ident[0:NC, 0:NC]).then_inc(base_ps, 1)
                pe.wait_ge(offset_ready, 1)
                for j in range(T):
                    mm = nc.tensor.transpose(bank[j // 4][:, j % 4 * NCP:j % 4 * NCP + NC], rel_c[:, j:CH:T], ident[0:NC, 0:NC])
                mm.then_inc(offset_ps, 1)
                pe.wait_ge(w_in, 192)
                nc.tensor.matmul(bank[6][:, 0:1], w1n[:, :], b2e_col[:, :], start=True, stop=True).then_inc(b1n_ps, 1)

            @block.vector
            def _(v):
                n = [0]

                def step(ins):
                    n[0] += 1
                    ins.then_inc(dve, 1)
                    v.wait_ge(dve, n[0])

                nc.vector.memset(x_sb[96:128, FULL, :], 0.0).then_inc(x_padded, 1)
                nc.vector.memset(ones_bf[:, :], 1.0)
                nc.vector.memset(zeros_bf[:, :], 0.0)
                nc.vector.memset(deg[:, :], 0.0)
                nc.vector.memset(rel[:, :, NC:NCP], MASKED)
                v.wait_ge(dst_in, 32)
                nc.vector.tensor_scalar(base_ci[:, :], dst_i[:, 0:1], -LOW, None, ALU.bitwise_and)
                step(nc.vector.tensor_copy(dst_f, dst_i))
                step(nc.vector.tensor_copy(base_c[:, :], base_ci[:, :]))
                step(nc.vector.tensor_scalar(rel_c, dst_f, base_c[:, 0:1], None, ALU.subtract))
                nc.vector.tensor_reduce(extreme[:, 0:1], rel_c, AX.X, ALU.min)
                step(nc.vector.tensor_reduce(extreme[:, 1:2], rel_c, AX.X, ALU.max))
                nc.vector.tensor_scalar(outside[:, 0:1], extreme[:, 0:1], 0.0, None, ALU.is_lt)
                nc.vector.tensor_scalar(outside[:, 1:2], extreme[:, 1:2], float(WIN), None, ALU.is_ge).then_inc(found, 1)
                v.wait_ge(total_ready, 1)
                step(nc.vector.tensor_scalar(fast[:, :], bank[4][:, 0:1], 0.0, None, ALU.is_equal))
                step(nc.vector.tensor_tensor(base_c[:, :], base_c[:, :], fast[0:NC, :], ALU.mult))
                nc.vector.tensor_scalar(rel_c, dst_f, base_c[:, 0:1], None, ALU.subtract).then_inc(offset_ready, 1)
                nc.vector.tensor_copy(base_all[:, :], base_c[:, :]).then_inc(base_ready, 1)
                step(nc.vector.tensor_scalar(npass_f[:, :], fast[:, :], float(1 - NWIN), float(NWIN), ALU.mult, ALU.add))
                nc.vector.tensor_copy(npass_i[:, :], npass_f[0:1, :])
                v.wait_ge(base_ps, 1)
                nc.vector.tensor_copy(base_f[:, :], bank[5][0:1, 0:NC])
                v.wait_ge(offset_ps, 1)
                for j in range(4):
                    ins = nc.vector.tensor_copy(rel[:, 4 * j:4 * j + 4, 0:NC],
                                                bank[j][:, 0:4 * NCP].rearrange("p (t c) -> p t c", t=4)[:, :, 0:NC])
                ins.then_inc(offset_copied, 1)
                v.wait_ge(consts, 5)
                nc.vector.tensor_tensor(fold[:, :], ident[:, 0:LOW], ident[:, LOW:2 * LOW], ALU.add).then_inc(dve, 1)
                n[0] += 1
                v.wait_ge(dve, n[0])
                step(nc.vector.tensor_tensor(fold[:, :], fold[:, :], ident[:, 2 * LOW:3 * LOW], ALU.add))
                nc.vector.tensor_tensor(fold[:, :], fold[:, :], ident[:, 3 * LOW:4 * LOW], ALU.add)
                v.wait_ge(w_in, 192)
                step(nc.vector.tensor_scalar(eps1[:, :], eps1[:, :], 1.0, None, ALU.add))
                b2e_tiled = b2e_b[0:1, :].unsqueeze(1).broadcast_to((1, GP, D))
                nc.vector.tensor_tensor(parts_f[:, 1, 0, :].rearrange("o (g d) -> o g d", d=D),
                                        parts_f[:, 1, 0, :].rearrange("o (g d) -> o g d", d=D), b2e_tiled, ALU.subtract)
                v.wait_ge(b1n_ps, 1)
                step(nc.vector.tensor_scalar(stat[:, 5, 0:1], bank[6][:, 0:1], eps1[:, 0:1], None, ALU.mult))
                step(nc.vector.tensor_tensor(b1n[:, :], b1n[:, :], stat[:, 5, 0:1], ALU.subtract))
                step(nc.vector.tensor_copy(parts[:, :, 0, :], parts_f[:, :, 0, :]))
                step(nc.vector.tensor_tensor(parts_f[:, :, 1, :], parts_f[:, :, 0, :], parts[:, :, 0, :], ALU.subtract))
                step(nc.vector.tensor_copy(parts[:, :, 1, :], parts_f[:, :, 1, :]))
                step(nc.vector.tensor_tensor(parts_f[:, :, 0, :], parts_f[:, :, 1, :], parts[:, :, 1, :], ALU.subtract))
                nc.vector.tensor_copy(parts[:, :, 2, :], parts_f[:, :, 0, :]).then_inc(parts_ready, 1)
                v.wait_ge(summed_x, 1)
                nc.vector.tensor_scalar(stat[:, 1, :], stat[:, 0, :], -1.0 / D, None, ALU.mult).then_inc(mean_ready, 1)
                v.wait_ge(summed_sq, 1)
                nc.vector.tensor_scalar(stat[:, 2, :], stat[:, 2, :], 1.0 / D, EPS_LN, ALU.mult, ALU.add).then_inc(rstd_ready, 1)
                v.wait_ge(std_ready, 1)
                step(nc.vector.reciprocal(stat[:, 3, :], stat[:, 2, :]))
                nc.vector.tensor_tensor(stat[:, 4, :], stat[:, 1, :], stat[:, 3, :], ALU.mult).then_inc(rstd_ready, 1)
                v.wait_ge(masked, 1)

        n_pass = nc.values_load(npass_i[0:1, 0:1], min_val=1, max_val=NWIN)
        with nc.Fori(0, n_pass) as _:
            degree_pass(nc, rel, base_all, rel_i, low_bf, high_bf, iota_rep, low_oh, high_oh, zeros_bf, counts,
                        counts_c, fold, where, where_iota, deg, bank)

        with ExitStack() as st:
            (dve, clipped, root_ready, spread, stored) = split_sems("dve_step2 clipped root_ready spread stored_rows", st)
            block = st.enter_context(nc.Block())

            @block.vector
            def _(v):
                nc.vector.tensor_scalar(deg[:, :], deg[:, :], 1.0, None, ALU.max).then_inc(clipped, 1)
                v.wait_ge(root_ready, 1)
                nc.vector.reciprocal(deg[:, :], deg[:, :]).then_inc(dve, 1)
                v.wait_ge(dve, 1)
                for q in range(NB // LOW):
                    cols = deg[:, q:NH:NB // LOW]
                    nc.vector.tensor_copy(rows[q * LOW:(q + 1) * LOW, :, 0:1], cols.unsqueeze(2)).then_inc(spread, 1)
                nc.vector.tensor_scalar(npass_f[:, :], npass_f[:, :], float(WIN), None, ALU.mult).then_inc(dve, 1)
                v.wait_ge(dve, 2)
                nc.vector.tensor_scalar(rel[:, :, :], rel[:, :, :], npass_f[:, 0:1], None, ALU.add)
                nc.vector.memset(acc[:, :], 0.0)

            @block.scalar
            def _(act):
                act.wait_ge(clipped, 1)
                nc.scalar.activation(deg[:, :], deg[:, :], ACT.Sqrt).then_inc(root_ready, 1)

            @block.sync
            def _(sp):
                sp.wait_ge(spread, NB // LOW)
                sp.dma_start(table[0:FULL * NB, :].rearrange("(k p) w -> p k w", p=NB), rows[:, 0:FULL, :]).then_inc(stored, 16)
                sp.dma_start(table[FULL * NB:N, :], rows[0:REST, FULL, :]).then_inc(stored, 16)
                sp.wait_ge(stored, 32)

        gathered = [sem(f"gathered{u}") for u in range(2)]
        with nc.Fori(0, n_pass) as p:
            edge_pass(nc, p, t, table, rel, base_f, base_i, a_sb, idx, aT, edge_rows, onehot, iota, w1e, bias_split,
                      ones_bf, w2e, ident, win_sb, rT_sb, acc, bank, gathered)

        with ExitStack() as st:
            (staged, turned, scaled, combined, combT_ps, combT_ready, hidden_ps, hidden_ready, mlp_ps, out_ready,
             squared, ms_ready, rms_ready, inverse, normed, y_ready, stored) = split_sems(
                "staged turned scaled_sums combined combT_ps combT_ready hidden_ps hidden_ready mlp_ps out_ready "
                "squared ms_ready rms_ready inverse normed_out y_ready stored_out", st)
            block = st.enter_context(nc.Block())
            G = 4
            GROUPS = -(-NBLK // G)

            def pair():
                ap = scratch(2 * G * NB)
                return ap.rearrange("p (u g n) -> p u g n", u=2, g=G)

            o2[0] = 0
            stage, comb, combT, hidT, squares = pair(), pair(), pair(), pair(), pair()
            turned_b, combT_b, hidden_b, mlp_b = [[bank[2 * i + u][:, :].rearrange("p (g n) -> p g n", g=G) for u in range(2)]
                                                  for i in range(4)]

            norm = sb("norm", [128, 3, 2, G])

            def blocks(s):
                return NBLK - s * G if s is GROUPS - 1 else G

            def cols(s):
                return bass.ds(s * G, blocks(s))

            def groups(eng, one):
                one(0, 0, True, False, False)
                one(1, 1, True, True, False)
                with eng.Fori(1, (GROUPS - 1) // 2) as i:
                    for u in range(2):
                        one(2 * i + u, u, True, True, True)
                one(GROUPS - 1, 0, True, True, True)
                one(GROUPS, 1, False, True, True)
                one(GROUPS + 1, 0, False, False, True)

            @block.scalar
            def _(act):
                def one(s, u, now, before, earlier):
                    if now:
                        n = blocks(s)
                        nc.scalar.activation(stage[:, u, 0:n, :].rearrange("p g n -> p (g n)"), acc[:, bass.ds(s * (G * NB), n * NB)],
                                             ACT.Copy).then_inc(staged, 1)
                    if before:
                        p = GROUPS - 1 if s is GROUPS else s - 1
                        act.wait_ge(out_ready, p + 1)
                        for g in range(blocks(p)):
                            blk = bass.ds(p * G + g, 1)
                            ins = nc.scalar.activation(squares[:, 1 - u, g, :], rows[:, blk, 1:ROW].rearrange("p o d -> p (o d)"),
                                                       ACT.Square, accum_out=norm[:, 0, 1 - u, g:g + 1])
                        ins.then_inc(squared, 1)
                    if now:
                        act.wait_ge(combT_ps, s + 1)
                        nc.scalar.activation(combT[:, u, 0:n, :], combT_b[u][:, 0:n, :], ACT.Copy).then_inc(combT_ready, 1)
                        act.wait_ge(hidden_ps, s + 1)
                        nc.scalar.activation(hidT[:, u, 0:n, :], hidden_b[u][:, 0:n, :], ACT.Relu,
                                             bias=b1n[:, 0:1]).then_inc(hidden_ready, 1)
                    if before:
                        act.wait_ge(ms_ready, p + 1)
                        nc.scalar.activation(norm[:, 1, 1 - u, 0:blocks(p)], norm[:, 1, 1 - u, 0:blocks(p)], ACT.Sqrt).then_inc(rms_ready, 1)
                groups(act, one)

            @block.tensor
            def _(pe):
                def one(s, u, now, before, earlier):
                    if now:
                        n = blocks(s)
                        pe.wait_ge(staged, s + 1)
                        for g in range(n):
                            mm = nc.tensor.transpose(turned_b[u][:, g, :], stage[:, u, g, :], ident[:, :])
                        mm.then_inc(turned, 1)
                    if before:
                        p = GROUPS - 1 if s is GROUPS else s - 1
                        pe.wait_ge(hidden_ready, p + 1)
                        if earlier and not s is GROUPS + 1 and not (isinstance(s, int) and s < 3):
                            pe.wait_ge(out_ready, p - 1)
                        m = blocks(p)
                        nc.tensor.matmul(mlp_b[1 - u][:, 0:m, :], ones_bf[:, :], bias_split[:, 1, 0:m * D], start=True, stop=False)
                        for g in range(m):
                            mm = nc.tensor.matmul(mlp_b[1 - u][:, g, :], hidT[:, 1 - u, g, :], w2n[:, :], start=False, stop=g == m - 1)
                        mm.then_inc(mlp_ps, 1)
                    if now:
                        pe.wait_ge(combined, s + 1)
                        for g in range(n):
                            mm = nc.tensor.transpose(combT_b[u][:, g, :], comb[:, u, g, :], ident[:, :])
                        mm.then_inc(combT_ps, 1)
                        pe.wait_ge(combT_ready, s + 1)
                        nc.tensor.matmul(hidden_b[u][:, 0:n, :], w1n[:, :], combT[:, u, 0:n, :], start=True, stop=True).then_inc(hidden_ps, 1)
                groups(pe, one)

            @block.vector
            def _(v):
                def one(s, u, now, before, earlier):
                    if now:
                        n = blocks(s)
                        v.wait_ge(turned, s + 1)
                        nc.vector.tensor_tensor(comb[:, u, 0:n, :], turned_b[u][:, 0:n, :],
                                                rows[:, cols(s), 0:1].broadcast_to((128, n, D)), ALU.mult).then_inc(scaled, 1)
                        v.wait_ge(scaled, s + 1)
                        nc.vector.scalar_tensor_tensor(out=comb[:, u, 0:n, :], in0=rows[:, cols(s), 1:ROW], scalar=eps1[:, 0:1],
                                                       in1=comb[:, u, 0:n, :], op0=ALU.mult, op1=ALU.add).then_inc(combined, 1)
                    if earlier:
                        e = GROUPS - 1 if s is GROUPS + 1 else s - 2
                        v.wait_ge(rms_ready, e + 1)
                        nc.vector.reciprocal(norm[:, 2, u, 0:blocks(e)], norm[:, 1, u, 0:blocks(e)]).then_inc(inverse, 1)
                        v.wait_ge(inverse, e + 1)
                        for g in range(blocks(e)):
                            blk = bass.ds(e * G + g, 1)
                            out = rows[:, blk, 1:ROW].rearrange("p o d -> p (o d)")
                            ins = nc.vector.scalar_tensor_tensor(out=out, in0=out, scalar=norm[:, 2, u, g:g + 1], in1=rmsw_b[:, :],
                                                                 op0=ALU.mult, op1=ALU.mult)
                        ins.then_inc(normed, 1)
                    if before:
                        p = GROUPS - 1 if s is GROUPS else s - 1
                        m = blocks(p)
                        v.wait_ge(mlp_ps, p + 1)
                        nc.vector.tensor_tensor(rows[:, cols(p), 1:ROW], mlp_b[1 - u][:, 0:m, :], rows[:, cols(p), 1:ROW],
                                                ALU.add).then_inc(out_ready, 1)
                        v.wait_ge(squared, p + 1)
                        nc.vector.tensor_scalar(norm[:, 1, 1 - u, 0:m], norm[:, 0, 1 - u, 0:m], 1.0 / D, EPS_RMS,
                                                ALU.mult, ALU.add).then_inc(ms_ready, 1)
                groups(v, one)

            @block.gpsimd
            def _(pool):
                def one(e):
                    pool.wait_ge(normed, e + 1)
                    nc.gpsimd.tensor_tensor(x_sb[:, cols(e), :], x_sb[:, cols(e), :], rows[:, cols(e), 1:ROW],
                                            ALU.add).then_inc(y_ready, 1)
                with pool.Fori(0, GROUPS - 1) as e:
                    one(e)
                one(GROUPS - 1)

            @block.sync
            def _(sp):
                with sp.Fori(0, GROUPS - 1) as e:
                    sp.wait_ge(y_ready, e + 1)
                    sp.dma_start(t["out"][bass.ds(e * (G * NB), G * NB), :].rearrange("(k p) d -> p k d", p=NB),
                                 x_sb[:, bass.ds(e * G, G), :]).then_inc(stored, 16)
                sp.wait_ge(y_ready, GROUPS)
                sp.dma_start(t["out"][FULL * NB:N, :], x_sb[0:REST, FULL, :]).then_inc(stored, 16)
                sp.wait_ge(stored, 16 * GROUPS)


def clear(nc, sems):
    nc.all_engine_barrier()
    for s in sems:
        nc.sync.sem_clear(s)
    nc.all_engine_barrier()


def degree_pass(nc, rel, base_all, rel_i, low_bf, high_bf, iota_rep, low_oh, high_oh, zeros_bf, counts,
                counts_c, fold, where, where_iota, deg, bank):
    with ExitStack() as st:
        names = "dve_step high_ready low_ready low_used counts_ready folded folded_ready where_ready placed"
        sems = [st.enter_context(nc.semaphore(n)) for n in names.split()]
        (dve, high_ready, low_ready, low_used, counts_ready, folded, folded_ready, where_ready, placed) = sems
        PC = QT * HIGH
        BC = 512 // PC

        with nc.Block() as block:
            @block.tensor
            def _(pe):
                banks = -(-NC // BC)
                for b in range(banks):
                    nc.tensor.matmul(bank[b][:, :], zeros_bf[:, 0:128], zeros_bf[:, :], start=True, stop=True)
                pe.wait_ge(high_ready, 1)
                for q in range(T // QT):
                    pe.wait_ge(low_ready, q + 1)
                    for c in range(NC):
                        at = c % BC * PC
                        mm = nc.tensor.matmul(
                            bank[c // BC][:, at:at + PC].rearrange("p (j h) -> p j h", h=HIGH),
                            low_oh[q % 2][:, :, :, c], high_oh[:, q * QT:(q + 1) * QT, :, c], start=False,
                            stop=q == T // QT - 1, skip_group_check=True)
                    mm.then_inc(low_used, 1)
                pe.wait_ge(counts_ready, 1)
                for h in range(HIGH):
                    mm = nc.tensor.matmul(bank[4][0:NC, h * LOW:(h + 1) * LOW], counts[:, h, :], fold[:, :], start=True, stop=True)
                mm.then_inc(folded, 1)
                pe.wait_ge(folded_ready, 1)
                pe.wait_ge(where_ready, 1)
                for h in range(HIGH):
                    mm = nc.tensor.matmul(bank[5][0:LOW, 0:NH], counts_c[:, h, :], where[:, HIGH - 1 - h:HIGH - 1 - h + NH],
                                          start=h == 0, stop=h == HIGH - 1)
                mm.then_inc(placed, 1)

            @block.vector
            def _(v):
                n = [0]

                def step(ins):
                    n[0] += 1
                    ins.then_inc(dve, 1)
                    v.wait_ge(dve, n[0])

                step(nc.vector.tensor_copy(rel_i, rel[:, :, :]))
                shift = LOW.bit_length() - 1
                step(nc.vector.tensor_scalar(low_oh_i(low_oh), rel_i, shift, None, ALU.arith_shift_right))
                step(nc.vector.tensor_scalar(rel_i, rel_i, LOW - 1, None, ALU.bitwise_and))
                nc.vector.tensor_copy(high_bf, low_oh_i(low_oh))
                step(nc.vector.tensor_copy(low_bf, rel_i))
                nc.vector.tensor_tensor(high_oh, high_bf.unsqueeze(2).broadcast_to((128, T, HIGH, NCP)),
                                        iota_rep[:, 0:HIGH, :].unsqueeze(1).broadcast_to((128, T, HIGH, NCP)),
                                        ALU.is_equal).then_inc(high_ready, 1)
                for q in range(T // QT):
                    if q >= 2:
                        v.wait_ge(low_used, q - 1)
                    for j in range(QT):
                        ins = nc.vector.tensor_tensor(
                            low_oh[q % 2][:, j, :, :], low_bf[:, q * QT + j, :].unsqueeze(1).broadcast_to((128, LOW, NCP)),
                            iota_rep, ALU.is_equal)
                    ins.then_inc(low_ready, 1)
                nc.vector.tensor_scalar(where[:, :], where_iota[:, :], base_all[:, 0:1], None, ALU.is_equal).then_inc(where_ready, 1)
                v.wait_ge(low_used, T // QT)
                for j in range(QT):
                    for b in range(-(-NC // BC)):
                        c0, c1 = b * BC, min(NC, b * BC + BC)
                        p = slice(j * LOW, (j + 1) * LOW)
                        ins = nc.vector.tensor_copy(
                            counts[p, :, c0:c1],
                            bank[b][p, 0:(c1 - c0) * PC].rearrange("p (c j h) -> p j h c", j=QT, h=HIGH)[:, j, :, :])
                ins.then_inc(counts_ready, 1)
                v.wait_ge(folded, 1)
                nc.vector.tensor_copy(counts_c, bank[4][0:NC, 0:HIGH * LOW].rearrange("p (h l) -> p h l", h=HIGH)).then_inc(folded_ready, 1)
                v.wait_ge(placed, 1)
                nc.vector.tensor_tensor(deg[:, :], deg[:, :], bank[5][0:LOW, 0:NH], ALU.add)
                nc.vector.tensor_scalar(rel[:, :, :], rel[:, :, :], float(-WIN), None, ALU.add)
                nc.vector.tensor_scalar(base_all[:, :], base_all[:, :], float(WIN), None, ALU.add)

        clear(nc, sems)


def low_oh_i(low_oh):
    return low_oh[0].rearrange("p t n c -> p (t n c)").bitcast(I32)[:, 0:T * NCP].rearrange("p (t c) -> p t c", t=T)


def edge_pass(nc, p, t, table, rel, base_f, base_i, a_sb, idx, aT, edge_rows, onehot, iota, w1e, bias_split,
              ones_bf, w2e, ident, win_sb, rT_sb, acc, bank, gathered):
    with ExitStack() as st:
        def sem(name):
            return st.enter_context(nc.semaphore(name))

        in_pass = [(LAST // 2 + 1) * T * 16, LAST // 2 * T * 16]
        before = [p * in_pass[u] for u in range(2)]
        starts_ready = sem("starts_ready")
        a_in = [sem(f"a_in{u}") for u in range(2)]
        idx_in = [sem(f"idx_in{u}") for u in range(2)]
        slot_free = sem("slot_free")
        aT_ps = sem("aT_ps")
        aT_ready = sem("aT_ready")
        z_ps = sem("z_ps")
        r_ready = sem("r_ready")
        onehot_ready = sem("onehot_ready")
        summed = sem("summed")
        win_ready = sem("win_ready")
        rT_ps = sem("rT_ps")
        rT_ready = sem("rT_ready")
        win_ps = sem("win_ps")
        added = sem("added")
        every = [starts_ready, *a_in, *idx_in, slot_free, aT_ps, aT_ready, z_ps, r_ready, onehot_ready, summed,
                 win_ready, rT_ps, rT_ready, win_ps, added]
        aT_bank = bank[0:2]
        z_bank = bank[2:4]
        sum_bank = [bank[4][:, 0:2 * D], bank[5][:, 0:2 * D]]
        rT_bank, win_bank = bank[6][:, 0:WIN], bank[7][:, 0:WIN]

        def chunks(eng, one):
            one(0, 0, 0)
            one(1, 1, 1)
            with eng.Fori(1, LAST // 2) as i:
                for u in range(2):
                    one(2 * i + u, u, 2)
            one(LAST, 0, 2)

        with nc.Block() as block:
            @block.sync
            def _(sp):
                def one(c, u, past):
                    start = TAIL0 if c is LAST else c * CH
                    if past == 2:
                        sp.wait_ge(gathered[u], before[u] + (c - u) * (8 * T))
                    sp.dma_start(idx[:, u, :], t["src"][bass.ds(start, CH)].rearrange("(p t) -> p t", t=T)).then_inc(idx_in[u], 16)
                    if past == 2:
                        sp.wait_ge(aT_ps, (c - 1) * NG)
                    sp.dma_start(a_sb[:, u, :, :], t["attr"][bass.ds(start, CH), :].rearrange("(p t) d -> p t d", t=T)).then_inc(a_in[u], 16)
                chunks(sp, one)

            @block.gpsimd
            def _(pool):
                def one(c, u, past):
                    pool.wait_ge(idx_in[u], (c - u) * 8 + 16)
                    if past == 2:
                        pool.wait_ge(summed, (c - 1) * NG)
                        pool.sem_inc(slot_free, 1)
                    for j in range(T):
                        nc.gpsimd.indirect_dma_start(
                            out=edge_rows[:, u, j, 0:ROW], out_offset=None, in_=table,
                            in_offset=bass.IndirectOffsetOnAxis(ap=idx[:, u, j:j + 1], axis=0)).then_inc(gathered[u], 16)
                chunks(pool, one)
                for u in range(2):
                    pool.wait_ge(gathered[u], before[u] + in_pass[u])

            @block.tensor
            def _(pe):
                def edge_mlp(q, slot, first):
                    pe.wait_ge(aT_ready, q + 1)
                    if not first:
                        pe.wait_ge(r_ready, q)
                    for odd in range(2):
                        nc.tensor.matmul(z_bank[odd][:, :], ones_bf[:, :], bias_split[:, 0, :], start=True, stop=False)
                    for j in range(GP):
                        for odd in range(2):
                            half = slice(odd * ED, odd * ED + ED)
                            mm = nc.tensor.matmul(z_bank[odd][:, j * D:(j + 1) * D], aT[half, slot, j, :],
                                                  w1e[half, :], start=False, stop=j == GP - 1)
                    mm.then_inc(z_ps, 1)

                def sum_group(c, u, g, first):
                    q = c * NG + g
                    pe.wait_ge(onehot_ready, q + 1)
                    pe.wait_ge(r_ready, q + 1)
                    if g == 0 and not first:
                        pe.wait_ge(win_ready, c - 1)
                    for j in range(GT):
                        k = g * GT + j
                        mm = nc.tensor.matmul(sum_bank[u], onehot[:, g % 2, j, :], edge_rows[:, u, k, 1:XW],
                                              start=k == 0, stop=k == T - 1)
                    mm.then_inc(summed, 1)

                def turn_relu(c):
                    pe.wait_ge(win_ready, c + 1)
                    nc.tensor.transpose(rT_bank, win_sb[:, D:2 * D], ident[:, :]).then_inc(rT_ps, 1)

                def window(c, first):
                    pe.wait_ge(rT_ready, c + 1)
                    if not first:
                        pe.wait_ge(added, c)
                    nc.tensor.matmul(win_bank, w2e[:, :], rT_sb[:, :], start=True, stop=False)
                    nc.tensor.matmul(win_bank, win_sb[:, 0:D], ident[:, :], start=False, stop=True).then_inc(win_ps, 1)

                def one(c, u, past):
                    for g in range(NG):
                        q = c * NG + g
                        if g == 0:
                            pe.wait_ge(a_in[u], (c - u) * 8 + 16)
                        if not (past == 0 and g < 2):
                            pe.wait_ge(aT_ready, q - 1)
                        for j in range(GP):
                            k = g * GT + 2 * j
                            mm = nc.tensor.transpose(aT_bank[g % 2][:, j * 128:(j + 1) * 128],
                                                     a_sb[:, u, k:k + 2, :].rearrange("p j d -> p (j d)"), ident[:, :])
                        mm.then_inc(aT_ps, 1)
                        if not (past == 0 and g == 0):
                            edge_mlp(q - 1, (g + 1) % 2, past == 0)
                        if past >= 1:
                            sum_group(c - 1, 1 - u, g, past < 2)
                        if past == 2 and g == 0:
                            turn_relu(c - 2)
                        if past == 2 and g == 1:
                            window(c - 2, False)
                one(0, 0, 0)
                one(1, 1, 1)
                with pe.Fori(1, LAST // 2) as i:
                    for u in range(2):
                        one(2 * i + u, u, 2)
                one(LAST, 0, 2)
                edge_mlp(NC * NG - 1, 1, False)
                for g in range(NG):
                    sum_group(LAST, 0, g, False)
                    if g == 0:
                        turn_relu(LAST - 1)
                window(LAST - 1, False)
                turn_relu(LAST)
                window(LAST, False)

            @block.scalar
            def _(act):
                def relu(c, u, g, free):
                    act.wait_ge(z_ps, c * NG + g + 1)
                    if g == 0 and free:
                        act.wait_ge(summed, (c - 1) * NG)
                    for odd in range(2):
                        ins = nc.scalar.activation(
                            edge_rows[:, u, g * GT + odd:(g + 1) * GT:2, ROW:XW],
                            z_bank[odd][:, :].rearrange("p (j d) -> p j d", d=D), ACT.Relu)
                    ins.then_inc(r_ready, 1)

                def one(c, u, past):
                    for g in range(NG):
                        q = c * NG + g
                        act.wait_ge(aT_ps, q + 1)
                        if not (past == 0 and g < 2):
                            act.wait_ge(z_ps, q - 1)
                        nc.scalar.activation(aT[:, g % 2, :, :],
                                             aT_bank[g % 2][:, :].rearrange("p (j n) -> p j n", n=128),
                                             ACT.Copy).then_inc(aT_ready, 1)
                        if g > 0:
                            relu(c, u, g - 1, past == 2)
                        elif past >= 1:
                            relu(c - 1, 1 - u, NG - 1, False)
                chunks(act, one)
                relu(LAST, 0, NG - 1, False)

            @block.vector
            def _(v):
                def read_sums(c, u):
                    v.wait_ge(summed, (c + 1) * NG)
                    nc.vector.tensor_copy(win_sb[:, :], sum_bank[u]).then_inc(win_ready, 1)

                def read_rT(c):
                    v.wait_ge(rT_ps, c + 1)
                    nc.vector.tensor_copy(rT_sb[:, :], rT_bank).then_inc(rT_ready, 1)

                def add_window(c, first):
                    base = v.value_load(base_i[0:1, c:c + 1] if isinstance(c, int) else base_i[0:1, bass.ds(c, 1)],
                                        min_val=0, max_val=N - 1)
                    v.wait_ge(win_ps, c + 1)
                    if not first:
                        v.wait_ge(added, c)
                    nc.vector.tensor_tensor(acc[:, bass.ds(base, WIN)], acc[:, bass.ds(base, WIN)], win_bank,
                                            ALU.add).then_inc(added, 1)

                nc.vector.tensor_copy(base_i[:, :], base_f[:, :]).then_inc(starts_ready, 1)
                v.wait_ge(starts_ready, 1)

                def one(c, u, past):
                    if past == 2:
                        add_window(c - 2, False)
                    v.wait_ge(gathered[u], before[u] + ((c - u) * (8 * T) + 16 * T))
                    for g in range(NG):
                        q = c * NG + g
                        if not (past == 0 and g < 2):
                            v.wait_ge(summed, q - 1)
                        for j in range(GT):
                            k = g * GT + j
                            s_edge = edge_rows[:, u, k, 0:1]
                            ins = nc.vector.tensor_scalar(onehot[:, g % 2, j, :], iota[:, :],
                                                          rel[:, k, bass.ds(c, 1)], s_edge, ALU.is_equal, ALU.mult)
                        ins.then_inc(onehot_ready, 1)
                        if past >= 1 and g == 0:
                            read_sums(c - 1, 1 - u)
                        if past >= 1 and g == 1:
                            read_rT(c - 1)
                one(0, 0, 0)
                one(1, 1, 1)
                with v.Fori(1, LAST // 2) as i:
                    for u in range(2):
                        one(2 * i + u, u, 2)
                one(LAST, 0, 2)
                add_window(LAST - 1, False)
                read_sums(LAST, 0)
                read_rT(LAST)
                add_window(LAST, False)
                nc.vector.tensor_scalar(base_f[:, :], base_f[:, :], float(WIN), None, ALU.add)
                nc.vector.tensor_scalar(rel[:, :, :], rel[:, :, :], float(-WIN), None, ALU.add)

        clear(nc, every)


def kernel(**inputs):
    import numpy as _np
    import concourse.bacc as _bacc
    from concourse import mybir as _mybir
    from concourse.bass_utils import run_bass_kernel_spmd as _run

    nc = _bacc.Bacc("TRN2", target_bir_lowering=False, num_devices=1)
    layout = {
        "x": ("x", (N, D)), "src": ("src", (E,)), "dst": ("dst", (E,)), "attr": ("edge_attr_64", (E, ED)),
        "W1n": ("L0_gnn_W1n", (D, D)), "b1n": ("L0_gnn_b1n", (1, D)), "W2n": ("L0_gnn_W2n", (D, D)),
        "b2n": ("L0_gnn_b2n", (1, D)), "W1e": ("L0_gnn_W1e", (ED, D)), "b1e": ("L0_gnn_b1e", (1, D)),
        "W2e": ("L0_gnn_W2e", (D, D)), "b2e": ("L0_gnn_b2e", (1, D)), "eps": ("L0_gnn_gin_eps", (1, 1)),
        "rms_w": ("L0_gnn_rms_w", (1, D)),
    }
    arrays, t = {}, {}
    for name, (given, shape) in layout.items():
        a = _np.ascontiguousarray(inputs[given]).reshape(shape)
        arrays[f"in_{name}"] = a
        t[name] = nc.dram_tensor(f"in_{name}", shape, _mybir.dt.from_np(a.dtype), kind="ExternalInput").ap()
    t["out"] = nc.dram_tensor("out", (N, D), F32, kind="ExternalOutput").ap()
    build(nc, t)
    r = _run(nc, [arrays], core_ids=[0])
    return r.results[0]["out"]
```

```python
import concourse.bass as bass
from concourse import mybir
from contextlib import ExitStack

F32 = mybir.dt.float32
BF16 = mybir.dt.bfloat16
I32 = mybir.dt.int32
ALU = mybir.AluOpType
ACT = mybir.ActivationFunctionType
AX = mybir.AxisListType

N, E, D, ED = 6250, 206250, 128, 64
NB = 128
NBLK = -(-N // NB)
FULL = N // NB
REST = N - FULL * NB
T = 16
GT = 8
GP = GT // 2
NG = T // GT
CH = 128 * T
NC = -(-E // CH)
LAST = NC - 1
TAIL0 = E - CH
TWICE = LAST * CH - TAIL0
WIN = 128
NWIN = -(-N // WIN)
NCP = NC + NC % 2
LOW = 32
HIGH = WIN // LOW
NH = -(-N // LOW)
QT = T // 4
QS = T // QT
PC = QT * HIGH
BC = 512 // PC
ROW = 1 + D
XW = ROW + D
SLICE = 7
ACCW = QT * LOW * NCP // 2
MASKED = -4096.0
EPS_LN = 1e-5
EPS_RMS = 1.1920929e-07


def build(nc, t):
    ctx = ExitStack()
    with ctx:
        def sb(name, shape, dt=F32):
            return ctx.enter_context(nc.sbuf_tensor(name, shape, dt))

        def sem(name, scope=ctx):
            return scope.enter_context(nc.semaphore(name))

        table = nc.dram_tensor("node_rows", (N, ROW), F32).ap()

        x_sb = sb("x_sb", [128, NBLK, D])
        rows = sb("rows", [128, NBLK, ROW])
        acc = sb("acc", [128, ACCW])
        edge_rows = sb("edge_rows", [128, 2, T, XW])
        rel = sb("rel", [128, T, NCP])
        base_f = sb("base_f", [1, NC])
        base_i = sb("base_i", [1, NC], I32)
        npass_i = sb("npass_i", [1, 1], I32)
        npass_f = sb("npass_f", [128, 1])
        fast = sb("fast", [128, 1])
        w1e = sb("w1e", [2 * ED, D])
        w2e = sb("w2e", [D, D])
        w1n = sb("w1n", [D, D])
        w2n = sb("w2n", [D, D])
        b1n = sb("b1n", [D, 1])
        b2e_col = sb("b2e_col", [D, 1])
        b2e_b = sb("b2e_b", [128, D])
        rmsw_b = sb("rmsw_b", [128, D])
        eps1 = sb("eps1", [128, 1])
        bias_split = sb("bias_split", [3, 2, GP * D], BF16)
        ones_bf = sb("ones_bf", [3, 128], BF16)
        zeros_bf = sb("zeros_bf", [1, 512], BF16)
        ident = sb("ident", [128, 128])
        iota = sb("iota", [128, WIN])
        ones = sb("ones", [128, 128])
        stat = sb("stat", [128, 6, NBLK])
        deg = sb("deg", [LOW, NH])
        base_c = sb("base_c", [NC, 1])
        base_all = sb("base_all", [NC, 1])
        base_ci = sb("base_ci", [NC, 1], I32)
        extreme = sb("extreme", [NC, 2])
        outside = sb("outside", [NC, 2])
        where = sb("where", [NC, NH + HIGH - 1])
        where_iota = sb("where_iota", [NC, NH + HIGH - 1])
        fold = sb("fold", [128, LOW])
        win_sb = sb("win_sb", [128, 2 * D])
        rT_sb = sb("rT_sb", [128, WIN])
        bank = [ctx.enter_context(nc.psum_tensor(f"bank{i}", [128, 512], F32)) for i in range(8)]

        work = sb("work", [128, ACCW])
        o = [0]

        def ring(*dims):
            size = 1
            for d in dims:
                size *= d
            o[0] += size
            return work[:, o[0] - size:o[0]]

        a_sb = ring(2, T, ED).rearrange("p (u t d) -> p u t d", u=2, t=T)
        onehot = ring(2, GT, WIN).rearrange("p (u t n) -> p u t n", u=2, t=GT)
        aT = ring(2, GP, 128).rearrange("p (u t n) -> p u t n", u=2, t=GP)
        idx = ring(2, T).bitcast(I32).rearrange("p (u t) -> p u t", u=2)

        dst_i = work[0:NC, 0:CH].bitcast(I32)
        dst_f = work[0:NC, CH:2 * CH]
        rel_c = acc[0:NC, 0:CH]
        parts_f = work[0:1, 2 * CH:2 * CH + 4 * GP * D].rearrange("p (b v d) -> p b v d", b=2, v=2)
        parts = acc[0:1, CH:CH + 3 * GP * D].bitcast(BF16).rearrange("p (b m d) -> p b m d", b=2, m=3)
        low_oh = [r[:, 0:QT * LOW * NCP // 2].bitcast(BF16).rearrange("p (t n c) -> p t n c", t=QT, n=LOW)
                  for r in (acc, work)]
        flat = edge_rows[:, :, :, :].rearrange("p u t w -> p (u t w)")
        o2 = [0]

        def scratch(words):
            o2[0] += words
            return flat[:, o2[0] - words:o2[0]]

        high_oh = scratch(T * HIGH * NCP // 2).bitcast(BF16).rearrange("p (t n c) -> p t n c", t=T, n=HIGH)
        iota_rep = scratch(LOW * NCP // 2).bitcast(BF16).rearrange("p (n c) -> p n c", n=LOW)
        low_bf = scratch(T * NCP // 2).bitcast(BF16).rearrange("p (t c) -> p t c", t=T)
        high_bf = scratch(T * NCP // 2).bitcast(BF16).rearrange("p (t c) -> p t c", t=T)
        rel_i = scratch(T * NCP).bitcast(I32).rearrange("p (t c) -> p t c", t=T)
        rel_high = low_oh[0].rearrange("p t n c -> p (t n c)").bitcast(I32)[:, 0:T * NCP].rearrange("p (t c) -> p t c", t=T)
        counts = low_oh[0].rearrange("p t n c -> p (t n c)").bitcast(F32)[:, 0:HIGH * NC].rearrange("p (h c) -> p h c", h=HIGH)
        counts_c = work[0:NC, 0:HIGH * LOW].rearrange("p (h l) -> p h l", h=HIGH)

        def split_sems(names, scope):
            return [sem(n, scope) for n in names.split()]

        with ExitStack() as st:
            (x_in, dst_in, w_in, bias_in, split_in, consts, dve, x_padded, summed_x, mean_ready, summed_sq,
             rstd_step, scale_ready, normed, found, total_ready, base_ready, base_ps, offset_ready, offset_ps,
             offset_copied, npass_ready, masked, b1n_ps, parts_ready, high_ready, low_ready, low_used, counts_ready,
             folded, folded_ready, placed, deg_step, deg_added) = split_sems(
                "x_in dst_in w_in bias_in split_in consts dve_step x_padded summed_x mean_ready summed_sq "
                "rstd_step scale_ready normed found total_ready base_ready base_ps offset_ready offset_ps "
                "offset_copied npass_ready masked b1n_ps parts_ready high_ready low_ready low_used counts_ready "
                "folded folded_ready placed deg_step deg_added", st)
            block = st.enter_context(nc.Block())

            @block.sync
            def _(sp):
                sp.dma_start(dst_i[LAST:NC, :], t["dst"][TAIL0:E].unsqueeze(0)).then_inc(dst_in, 16)
                sp.dma_start(dst_i[0:LAST, :], t["dst"][0:LAST * CH].rearrange("(c e) -> c e", e=CH)).then_inc(dst_in, 16)
                for to, of in [
                    (parts_f[:, 0, 0, :].rearrange("o (g d) -> o g d", d=D), t["b1e"].unsqueeze(1).broadcast_to((1, GP, D))),
                    (parts_f[:, 1, 0, :].rearrange("o (g d) -> o g d", d=D), t["b2n"].unsqueeze(1).broadcast_to((1, GP, D))),
                    (b2e_b[:, :], t["b2e"].broadcast_to((128, D))),
                ]:
                    sp.dma_start(to, of).then_inc(bias_in, 16)
                weights = [
                    (w1n[:, :], t["W1n"]), (b2e_col[:, :], t["b2e"].rearrange("o d -> d o")),
                    (eps1[:, :], t["eps"].broadcast_to((128, 1))), (b1n[:, :], t["b1n"].rearrange("o d -> d o")),
                    (w1e[0:ED, :], t["W1e"]), (w1e[ED:2 * ED, :], t["W1e"]), (w2e[:, :], t["W2e"]),
                    (w2n[:, :], t["W2n"]), (rmsw_b[:, :], t["rms_w"].broadcast_to((128, D))),
                ]
                for to, of in weights:
                    sp.dma_start(to, of).then_inc(w_in, 16)
                sp.wait_ge(parts_ready, 1)
                for b in range(2):
                    sp.dma_start(bias_split[:, b, :], parts[:, b, :, :]).then_inc(split_in, 16)
                sp.wait_ge(split_in, 32)
                sp.wait_ge(w_in, 16 * len(weights))

            @block.scalar
            def _(act):
                act.wait_ge(x_padded, 1)
                act.dma_start(x_sb[:, 0:FULL, :], t["x"][0:FULL * NB, :].rearrange("(k p) d -> p k d", p=NB)).then_inc(x_in, 16)
                act.dma_start(x_sb[0:REST, FULL, :], t["x"][FULL * NB:N, :]).then_inc(x_in, 16)
                act.wait_ge(x_in, 32)
                for k in range(NBLK):
                    ins = nc.scalar.activation(rows[:, k, 1:ROW], x_sb[:, k, :], ACT.Copy, accum_out=stat[:, 0, k:k + 1])
                ins.then_inc(summed_x, 1)
                act.wait_ge(mean_ready, 1)
                for k in range(NBLK):
                    ins = nc.scalar.activation(rows[:, k, 1:ROW], x_sb[:, k, :], ACT.Square, bias=stat[:, 1, k:k + 1],
                                               accum_out=stat[:, 2, k:k + 1])
                ins.then_inc(summed_sq, 1)
                act.wait_ge(scale_ready, 1)
                for k in range(NBLK):
                    ins = nc.scalar.activation(rows[:, k, 1:ROW], x_sb[:, k, :], ACT.Relu, bias=stat[:, 4, k:k + 1],
                                               scale=stat[:, 3, k:k + 1])
                    if k % SLICE == SLICE - 1:
                        ins.then_inc(normed, 1)

            @block.gpsimd
            def _(pool):
                nc.gpsimd.memset(ones[:, :], 1.0).then_inc(consts, 1)
                nc.gpsimd.iota(iota[:, :], pattern=[[1, WIN]], base=0, channel_multiplier=0,
                               allow_small_or_imprecise_dtypes=True).then_inc(consts, 1)
                nc.gpsimd.iota(iota_rep, pattern=[[1, LOW], [0, NCP]], base=0, channel_multiplier=0,
                               allow_small_or_imprecise_dtypes=True).then_inc(consts, 1)
                nc.gpsimd.iota(where_iota[:, :], pattern=[[LOW, NH + HIGH - 1]], base=-LOW * (HIGH - 1),
                               channel_multiplier=0, allow_small_or_imprecise_dtypes=True).then_inc(consts, 1)
                pool.wait_ge(consts, 4)
                nc.gpsimd.affine_select(out=ident[:, :], in_=ones[:, :], compare_op=ALU.is_equal, fill=0.0, base=0,
                                        pattern=[[-1, 128]], channel_multiplier=1).then_inc(consts, 1)
                pool.wait_ge(offset_copied, 1)
                nc.gpsimd.affine_select(out=rel[:, :, LAST], in_=rel[:, :, LAST], compare_op=ALU.is_ge,
                                        fill=MASKED, base=-TWICE, pattern=[[1, T]],
                                        channel_multiplier=T).then_inc(masked, 1)
                m = [0]

                def pool_step(ins):
                    m[0] += 1
                    ins.then_inc(rstd_step, 1)
                    pool.wait_ge(rstd_step, m[0])

                pool_step(nc.gpsimd.memset(stat[:, 5, :], -0.5))
                pool.wait_ge(summed_x, 1)
                nc.gpsimd.tensor_scalar(stat[:, 1, :], stat[:, 0, :], -1.0 / D, None, ALU.mult).then_inc(mean_ready, 1)
                pool.wait_ge(summed_sq, 1)
                pool_step(nc.gpsimd.tensor_scalar(stat[:, 2, :], stat[:, 2, :], 1.0 / D, EPS_LN, ALU.mult, ALU.add))
                pool_step(nc.gpsimd.tensor_tensor(stat[:, 3, :], stat[:, 2, :], stat[:, 5, :], ALU.pow))
                pool_step(nc.gpsimd.tensor_tensor(stat[:, 4, :], stat[:, 3, :], stat[:, 3, :], ALU.mult))
                pool_step(nc.gpsimd.tensor_tensor(stat[:, 4, :], stat[:, 4, :], stat[:, 2, :], ALU.mult))
                pool_step(nc.gpsimd.tensor_scalar(stat[:, 4, :], stat[:, 4, :], -0.5, 1.5, ALU.mult, ALU.add))
                pool_step(nc.gpsimd.tensor_tensor(stat[:, 3, :], stat[:, 3, :], stat[:, 4, :], ALU.mult))
                nc.gpsimd.tensor_tensor(stat[:, 4, :], stat[:, 1, :], stat[:, 3, :], ALU.mult).then_inc(scale_ready, 1)
                pool.wait_ge(bias_in, 48)
                for k in range(0, NBLK, SLICE):
                    n = min(SLICE, NBLK - k)
                    pool.wait_ge(normed, k // SLICE + 1)
                    nc.gpsimd.tensor_tensor(rows[:, k:k + n, 1:ROW], rows[:, k:k + n, 1:ROW],
                                            b2e_b[:, :].unsqueeze(1).broadcast_to((128, n, D)), ALU.add)

            @block.tensor
            def _(pe):
                pe.wait_ge(consts, 5)
                pe.wait_ge(found, 1)
                for j in range(2):
                    mm = nc.tensor.matmul(bank[4][:, 0:1], ones[0:NC, :], outside[:, j:j + 1], start=j == 0, stop=j == 1)
                mm.then_inc(total_ready, 1)
                pe.wait_ge(base_ready, 1)
                nc.tensor.transpose(bank[5][0:1, 0:NC], base_c[:, :], ident[0:NC, 0:NC]).then_inc(base_ps, 1)
                pe.wait_ge(offset_ready, 1)
                for j in range(T):
                    mm = nc.tensor.transpose(bank[j // 4][:, j % 4 * NCP:j % 4 * NCP + NC], rel_c[:, j:CH:T], ident[0:NC, 0:NC])
                mm.then_inc(offset_ps, 1)
                pe.wait_ge(w_in, 16 * 9)
                nc.tensor.matmul(bank[6][:, 0:1], w1n[:, :], b2e_col[:, :], start=True, stop=True).then_inc(b1n_ps, 1)

                def degree_pass(p):
                    for b in range(-(-NC // BC)):
                        nc.tensor.matmul(bank[b][:, :], zeros_bf[:, 0:128], zeros_bf[:, :], start=True, stop=True)
                    pe.wait_ge(high_ready, p + 1)
                    for q in range(QS):
                        pe.wait_ge(low_ready, p * QS + (q + 1))
                        for c in range(NC):
                            at = c % BC * PC
                            mm = nc.tensor.matmul(
                                bank[c // BC][:, at:at + PC].rearrange("p (j h) -> p j h", h=HIGH),
                                low_oh[q % 2][:, :, :, c], high_oh[:, q * QT:(q + 1) * QT, :, c], start=False,
                                stop=q == QS - 1, skip_group_check=True)
                        mm.then_inc(low_used, 1)
                    pe.wait_ge(counts_ready, p + 1)
                    for h in range(HIGH):
                        mm = nc.tensor.matmul(bank[4][0:NC, h * LOW:(h + 1) * LOW], counts[:, h, :], fold[:, :], start=True, stop=True)
                    mm.then_inc(folded, 1)
                    pe.wait_ge(folded_ready, p + 1)
                    for h in range(HIGH):
                        mm = nc.tensor.matmul(bank[5][0:LOW, 0:NH], counts_c[:, h, :], where[:, HIGH - 1 - h:HIGH - 1 - h + NH],
                                              start=h == 0, stop=h == HIGH - 1)
                    mm.then_inc(placed, 1)

                pe.wait_ge(npass_ready, 1)
                n_pass = pe.value_load(npass_i[0:1, 0:1], min_val=1, max_val=NWIN)
                pe.wait_ge(offset_copied, 1)
                with pe.Fori(0, n_pass) as p:
                    degree_pass(p)

            @block.vector
            def _(v):
                n = [0]

                def step(ins):
                    n[0] += 1
                    ins.then_inc(dve, 1)
                    v.wait_ge(dve, n[0])

                nc.vector.memset(x_sb[96:128, FULL, :], 0.0).then_inc(x_padded, 1)
                nc.vector.memset(ones_bf[:, :], 1.0)
                nc.vector.memset(zeros_bf[:, :], 0.0)
                nc.vector.memset(deg[:, :], 0.0)
                nc.vector.memset(rel[:, :, NC:NCP], MASKED)
                v.wait_ge(bias_in, 48)
                b2e_tiled = b2e_b[0:1, :].unsqueeze(1).broadcast_to((1, GP, D))
                step(nc.vector.tensor_tensor(parts_f[:, 1, 0, :].rearrange("o (g d) -> o g d", d=D),
                                             parts_f[:, 1, 0, :].rearrange("o (g d) -> o g d", d=D), b2e_tiled, ALU.subtract))
                step(nc.vector.tensor_copy(parts[:, :, 0, :], parts_f[:, :, 0, :]))
                step(nc.vector.tensor_tensor(parts_f[:, :, 1, :], parts_f[:, :, 0, :], parts[:, :, 0, :], ALU.subtract))
                step(nc.vector.tensor_copy(parts[:, :, 1, :], parts_f[:, :, 1, :]))
                step(nc.vector.tensor_tensor(parts_f[:, :, 0, :], parts_f[:, :, 1, :], parts[:, :, 1, :], ALU.subtract))
                nc.vector.tensor_copy(parts[:, :, 2, :], parts_f[:, :, 0, :]).then_inc(parts_ready, 1)
                v.wait_ge(consts, 5)
                step(nc.vector.tensor_tensor(fold[:, :], ident[:, 0:LOW], ident[:, LOW:2 * LOW], ALU.add))
                step(nc.vector.tensor_tensor(fold[:, :], fold[:, :], ident[:, 2 * LOW:3 * LOW], ALU.add))
                nc.vector.tensor_tensor(fold[:, :], fold[:, :], ident[:, 3 * LOW:4 * LOW], ALU.add)
                v.wait_ge(dst_in, 32)
                nc.vector.tensor_scalar(base_ci[:, :], dst_i[:, 0:1], -LOW, None, ALU.bitwise_and)
                step(nc.vector.tensor_copy(dst_f, dst_i))
                step(nc.vector.tensor_copy(base_c[:, :], base_ci[:, :]))
                step(nc.vector.tensor_scalar(rel_c, dst_f, base_c[:, 0:1], None, ALU.subtract))
                nc.vector.tensor_reduce(extreme[:, 0:1], rel_c, AX.X, ALU.min)
                step(nc.vector.tensor_reduce(extreme[:, 1:2], rel_c, AX.X, ALU.max))
                nc.vector.tensor_scalar(outside[:, 0:1], extreme[:, 0:1], 0.0, None, ALU.is_lt)
                nc.vector.tensor_scalar(outside[:, 1:2], extreme[:, 1:2], float(WIN), None, ALU.is_ge).then_inc(found, 1)
                v.wait_ge(total_ready, 1)
                step(nc.vector.tensor_scalar(fast[:, :], bank[4][:, 0:1], 0.0, None, ALU.is_equal))
                step(nc.vector.tensor_tensor(base_c[:, :], base_c[:, :], fast[0:NC, :], ALU.mult))
                nc.vector.tensor_scalar(rel_c, dst_f, base_c[:, 0:1], None, ALU.subtract).then_inc(offset_ready, 1)
                nc.vector.tensor_copy(base_all[:, :], base_c[:, :]).then_inc(base_ready, 1)
                step(nc.vector.tensor_scalar(npass_f[:, :], fast[:, :], float(1 - NWIN), float(NWIN), ALU.mult, ALU.add))
                nc.vector.tensor_copy(npass_i[:, :], npass_f[0:1, :]).then_inc(npass_ready, 1)
                v.wait_ge(base_ps, 1)
                nc.vector.tensor_copy(base_f[:, :], bank[5][0:1, 0:NC])
                v.wait_ge(offset_ps, 1)
                for j in range(4):
                    ins = nc.vector.tensor_copy(rel[:, 4 * j:4 * j + 4, 0:NC],
                                                bank[j][:, 0:4 * NCP].rearrange("p (t c) -> p t c", t=4)[:, :, 0:NC])
                ins.then_inc(offset_copied, 1)

                def degree_pass(p):
                    m = [0]

                    def pass_step(ins):
                        m[0] += 1
                        ins.then_inc(deg_step, 1)
                        v.wait_ge(deg_step, p * 4 + m[0])

                    pass_step(nc.vector.tensor_copy(rel_i, rel[:, :, :]))
                    pass_step(nc.vector.tensor_scalar(rel_high, rel_i, LOW.bit_length() - 1, None, ALU.arith_shift_right))
                    pass_step(nc.vector.tensor_scalar(rel_i, rel_i, LOW - 1, None, ALU.bitwise_and))
                    nc.vector.tensor_copy(high_bf, rel_high)
                    pass_step(nc.vector.tensor_copy(low_bf, rel_i))
                    nc.vector.tensor_tensor(high_oh, high_bf.unsqueeze(2).broadcast_to((128, T, HIGH, NCP)),
                                            iota_rep[:, 0:HIGH, :].unsqueeze(1).broadcast_to((128, T, HIGH, NCP)),
                                            ALU.is_equal).then_inc(high_ready, 1)
                    for q in range(QS):
                        if q >= 2:
                            v.wait_ge(low_used, p * QS + (q - 1))
                        for j in range(QT):
                            ins = nc.vector.tensor_tensor(
                                low_oh[q % 2][:, j, :, :], low_bf[:, q * QT + j, :].unsqueeze(1).broadcast_to((128, LOW, NCP)),
                                iota_rep, ALU.is_equal)
                        ins.then_inc(low_ready, 1)
                    nc.vector.tensor_scalar(where[:, :], where_iota[:, :], base_all[:, 0:1], None, ALU.is_equal)
                    v.wait_ge(low_used, p * QS + QS)
                    for j in range(QT):
                        for b in range(-(-NC // BC)):
                            c0, c1 = b * BC, min(NC, b * BC + BC)
                            lows = slice(j * LOW, (j + 1) * LOW)
                            ins = nc.vector.tensor_copy(
                                counts[lows, :, c0:c1],
                                bank[b][lows, 0:(c1 - c0) * PC].rearrange("p (c j h) -> p j h c", j=QT, h=HIGH)[:, j, :, :])
                    ins.then_inc(counts_ready, 1)
                    v.wait_ge(folded, p + 1)
                    nc.vector.tensor_copy(counts_c, bank[4][0:NC, 0:HIGH * LOW].rearrange("p (h l) -> p h l", h=HIGH)).then_inc(folded_ready, 1)
                    nc.vector.tensor_scalar(rel[:, :, :], rel[:, :, :], float(-WIN), None, ALU.add)
                    nc.vector.tensor_scalar(base_all[:, :], base_all[:, :], float(WIN), None, ALU.add)
                    v.wait_ge(placed, p + 1)
                    nc.vector.tensor_tensor(deg[:, :], deg[:, :], bank[5][0:LOW, 0:NH], ALU.add).then_inc(deg_added, 1)
                    v.wait_ge(deg_added, p + 1)

                v.wait_ge(split_in, 32)
                v.wait_ge(masked, 1)
                v.wait_ge(npass_ready, 1)
                n_pass = v.value_load(npass_i[0:1, 0:1], min_val=1, max_val=NWIN)
                with v.Fori(0, n_pass) as p:
                    degree_pass(p)

        with ExitStack() as st:
            (dve, clipped, root_ready, spread, stored) = split_sems("dve_step2 clipped root_ready spread stored_rows", st)
            block = st.enter_context(nc.Block())

            @block.vector
            def _(v):
                nc.vector.tensor_scalar(deg[:, :], deg[:, :], 1.0, None, ALU.max).then_inc(clipped, 1)
                v.wait_ge(root_ready, 1)
                nc.vector.reciprocal(deg[:, :], deg[:, :]).then_inc(dve, 1)
                v.wait_ge(dve, 1)
                for q in range(NB // LOW):
                    cols = deg[:, q:NH:NB // LOW]
                    nc.vector.tensor_copy(rows[q * LOW:(q + 1) * LOW, :, 0:1], cols.unsqueeze(2)).then_inc(spread, 1)
                nc.vector.tensor_scalar(eps1[:, :], eps1[:, :], 1.0, None, ALU.add).then_inc(dve, 1)
                v.wait_ge(dve, 2)
                nc.vector.tensor_scalar(stat[:, 5, 0:1], bank[6][:, 0:1], eps1[:, 0:1], None, ALU.mult).then_inc(dve, 1)
                v.wait_ge(dve, 3)
                nc.vector.tensor_tensor(b1n[:, :], b1n[:, :], stat[:, 5, 0:1], ALU.subtract)
                nc.vector.tensor_scalar(npass_f[:, :], npass_f[:, :], float(WIN), None, ALU.mult).then_inc(dve, 1)
                v.wait_ge(dve, 4)
                nc.vector.tensor_scalar(rel[:, :, :], rel[:, :, :], npass_f[:, 0:1], None, ALU.add)

            @block.gpsimd
            def _(pool):
                nc.gpsimd.memset(acc[:, :], 0.0)

            @block.scalar
            def _(act):
                act.wait_ge(clipped, 1)
                nc.scalar.activation(deg[:, :], deg[:, :], ACT.Sqrt).then_inc(root_ready, 1)

            @block.sync
            def _(sp):
                sp.wait_ge(spread, NB // LOW)
                sp.dma_start(table[0:FULL * NB, :].rearrange("(k p) w -> p k w", p=NB), rows[:, 0:FULL, :]).then_inc(stored, 16)
                sp.dma_start(table[FULL * NB:N, :], rows[0:REST, FULL, :]).then_inc(stored, 16)
                sp.wait_ge(stored, 32)

        n_pass = nc.values_load(npass_i[0:1, 0:1], min_val=1, max_val=NWIN)
        with nc.Fori(0, n_pass) as _:
            edge_pass(nc, t, table, rel, base_f, base_i, a_sb, idx, aT, edge_rows, onehot, iota, w1e, bias_split,
                      ones_bf, w2e, ident, win_sb, rT_sb, acc, bank)

        with ExitStack() as st:
            (staged, turned, scaled, combined, combT_ps, combT_ready, hidden_ps, hidden_ready, mlp_ps, out_ready,
             squared, ms_ready, rms_ready, inverse, normed, y_ready, stored) = split_sems(
                "staged turned scaled_sums combined combT_ps combT_ready hidden_ps hidden_ready mlp_ps out_ready "
                "squared ms_ready rms_ready inverse normed_out y_ready stored_out", st)
            block = st.enter_context(nc.Block())
            G = 4
            GROUPS = -(-NBLK // G)

            def pair():
                ap = scratch(2 * G * NB)
                return ap.rearrange("p (u g n) -> p u g n", u=2, g=G)

            o2[0] = 0
            stage, comb, combT, hidT, squares = pair(), pair(), pair(), pair(), pair()
            turned_b, combT_b, hidden_b, mlp_b = [[bank[2 * i + u][:, :].rearrange("p (g n) -> p g n", g=G) for u in range(2)]
                                                  for i in range(4)]

            norm = sb("norm", [128, 3, 2, G])

            def blocks(e):
                return NBLK - e * G if isinstance(e, int) and e == GROUPS - 1 else G

            def cols(e):
                return bass.ds(e * G, blocks(e))

            def live(e):
                return not isinstance(e, int) or 0 <= e < GROUPS

            LAG = 3
            LOOP = (2, (GROUPS - 2) // 2)

            def steps(eng, one):
                for s in range(2 * LOOP[0]):
                    one(s, s % 2)
                with eng.Fori(*LOOP) as i:
                    for u in range(2):
                        one(2 * i + u, u)
                for s in range(2 * LOOP[1], GROUPS + LAG):
                    one(s, s % 2)

            @block.scalar
            def _(act):
                def to_stage(e, u):
                    n = blocks(e)
                    nc.scalar.activation(stage[:, u, 0:n, :].rearrange("p g n -> p (g n)"), acc[:, bass.ds(e * (G * NB), n * NB)],
                                         ACT.Copy).then_inc(staged, 1)

                def one(s, u):
                    if live(s - 2):
                        e = s - 2
                        act.wait_ge(out_ready, e + 1)
                        for g in range(blocks(e)):
                            blk = bass.ds(e * G + g, 1)
                            ins = nc.scalar.activation(squares[:, u, g, :], rows[:, blk, 1:ROW].rearrange("p o d -> p (o d)"),
                                                       ACT.Square, accum_out=norm[:, 0, u, g:g + 1])
                        ins.then_inc(squared, 1)
                    if live(s - 1):
                        n = blocks(s - 1)
                        act.wait_ge(hidden_ps, s)
                        nc.scalar.activation(hidT[:, 1 - u, 0:n, :], hidden_b[1 - u][:, 0:n, :], ACT.Relu,
                                             bias=b1n[:, 0:1]).then_inc(hidden_ready, 1)
                    if live(s):
                        n = blocks(s)
                        act.wait_ge(combT_ps, s + 1)
                        nc.scalar.activation(combT[:, u, 0:n, :], combT_b[u][:, 0:n, :], ACT.Copy).then_inc(combT_ready, 1)
                    if live(s + 1):
                        to_stage(s + 1, 1 - u)
                    if live(s - 2):
                        act.wait_ge(ms_ready, s - 1)
                        nc.scalar.activation(norm[:, 1, u, 0:blocks(s - 2)], norm[:, 1, u, 0:blocks(s - 2)], ACT.Sqrt).then_inc(rms_ready, 1)
                to_stage(0, 0)
                steps(act, one)

            @block.tensor
            def _(pe):
                def one(s, u):
                    if live(s):
                        pe.wait_ge(staged, s + 1)
                        for g in range(blocks(s)):
                            mm = nc.tensor.transpose(turned_b[u][:, g, :], stage[:, u, g, :], ident[:, :])
                        mm.then_inc(turned, 1)
                    if live(s - 1):
                        m = blocks(s - 1)
                        pe.wait_ge(combT_ready, s)
                        nc.tensor.matmul(hidden_b[1 - u][:, 0:m, :], w1n[:, :], combT[:, 1 - u, 0:m, :], start=True,
                                         stop=True).then_inc(hidden_ps, 1)
                    if live(s):
                        pe.wait_ge(combined, s + 1)
                        for g in range(blocks(s)):
                            mm = nc.tensor.transpose(combT_b[u][:, g, :], comb[:, u, g, :], ident[:, :])
                        mm.then_inc(combT_ps, 1)
                    if live(s - 1):
                        pe.wait_ge(hidden_ready, s)
                        if not (isinstance(s, int) and s < 3):
                            pe.wait_ge(out_ready, s - 2)
                        nc.tensor.matmul(mlp_b[1 - u][:, 0:m, :], ones_bf[:, :], bias_split[:, 1, 0:m * D], start=True, stop=False)
                        for g in range(m):
                            mm = nc.tensor.matmul(mlp_b[1 - u][:, g, :], hidT[:, 1 - u, g, :], w2n[:, :], start=False, stop=g == m - 1)
                        mm.then_inc(mlp_ps, 1)
                steps(pe, one)

            @block.vector
            def _(v):
                def one(s, u):
                    if live(s - 2):
                        m = blocks(s - 2)
                        v.wait_ge(mlp_ps, s - 1)
                        nc.vector.tensor_tensor(rows[:, cols(s - 2), 1:ROW], mlp_b[u][:, 0:m, :], rows[:, cols(s - 2), 1:ROW],
                                                ALU.add).then_inc(out_ready, 1)
                    if live(s):
                        n = blocks(s)
                        v.wait_ge(turned, s + 1)
                        nc.vector.tensor_tensor(comb[:, u, 0:n, :], turned_b[u][:, 0:n, :],
                                                rows[:, cols(s), 0:1].broadcast_to((128, n, D)), ALU.mult).then_inc(scaled, 1)
                        v.wait_ge(scaled, s + 1)
                        nc.vector.scalar_tensor_tensor(out=comb[:, u, 0:n, :], in0=rows[:, cols(s), 1:ROW], scalar=eps1[:, 0:1],
                                                       in1=comb[:, u, 0:n, :], op0=ALU.mult, op1=ALU.add).then_inc(combined, 1)
                    if live(s - 2):
                        v.wait_ge(squared, s - 1)
                        nc.vector.tensor_scalar(norm[:, 1, u, 0:m], norm[:, 0, u, 0:m], 1.0 / D, EPS_RMS,
                                                ALU.mult, ALU.add).then_inc(ms_ready, 1)
                    if live(s - LAG):
                        e = s - LAG
                        v.wait_ge(rms_ready, e + 1)
                        nc.vector.reciprocal(norm[:, 2, 1 - u, 0:blocks(e)], norm[:, 1, 1 - u, 0:blocks(e)]).then_inc(inverse, 1)
                        v.wait_ge(inverse, e + 1)
                        for g in range(blocks(e)):
                            blk = bass.ds(e * G + g, 1)
                            out = rows[:, blk, 1:ROW].rearrange("p o d -> p (o d)")
                            ins = nc.vector.scalar_tensor_tensor(out=out, in0=out, scalar=norm[:, 2, 1 - u, g:g + 1], in1=rmsw_b[:, :],
                                                                 op0=ALU.mult, op1=ALU.mult)
                        ins.then_inc(normed, 1)
                steps(v, one)

            @block.gpsimd
            def _(pool):
                def one(e):
                    pool.wait_ge(normed, e + 1)
                    nc.gpsimd.tensor_tensor(x_sb[:, cols(e), :], x_sb[:, cols(e), :], rows[:, cols(e), 1:ROW],
                                            ALU.add).then_inc(y_ready, 1)
                with pool.Fori(0, GROUPS - 1) as e:
                    one(e)
                one(GROUPS - 1)

            @block.sync
            def _(sp):
                with sp.Fori(0, GROUPS - 1) as e:
                    sp.wait_ge(y_ready, e + 1)
                    sp.dma_start(t["out"][bass.ds(e * (G * NB), G * NB), :].rearrange("(k p) d -> p k d", p=NB),
                                 x_sb[:, bass.ds(e * G, G), :]).then_inc(stored, 16)
                sp.wait_ge(y_ready, GROUPS)
                sp.dma_start(t["out"][FULL * NB:N, :], x_sb[0:REST, FULL, :]).then_inc(stored, 16)
                sp.wait_ge(stored, 16 * GROUPS)


def clear(nc, sems):
    nc.all_engine_barrier()
    for s in sems:
        nc.sync.sem_clear(s)
    nc.all_engine_barrier()


def edge_pass(nc, t, table, rel, base_f, base_i, a_sb, idx, aT, edge_rows, onehot, iota, w1e, bias_split,
              ones_bf, w2e, ident, win_sb, rT_sb, acc, bank):
    with ExitStack() as st:
        def sem(name):
            return st.enter_context(nc.semaphore(name))

        starts_ready = sem("starts_ready")
        a_in = [sem(f"a_in{u}") for u in range(2)]
        idx_in = [sem(f"idx_in{u}") for u in range(2)]
        gathered = [[sem(f"gathered{u}{g}") for g in range(NG)] for u in range(2)]
        slot_free = sem("slot_free")
        aT_ps = sem("aT_ps")
        aT_ready = sem("aT_ready")
        z_ps = sem("z_ps")
        r_ready = sem("r_ready")
        onehot_ready = sem("onehot_ready")
        summed = sem("summed")
        win_ready = sem("win_ready")
        rT_ps = sem("rT_ps")
        rT_ready = sem("rT_ready")
        win_ps = sem("win_ps")
        added = sem("added")
        every = [starts_ready, *a_in, *idx_in, *gathered[0], *gathered[1], slot_free, aT_ps, aT_ready, z_ps, r_ready, onehot_ready, summed,
                 win_ready, rT_ps, rT_ready, win_ps, added]
        aT_bank = bank[0:2]
        z_bank = bank[2:4]
        sum_bank = [bank[4][:, 0:2 * D], bank[5][:, 0:2 * D]]
        rT_bank, win_bank = bank[6][:, 0:WIN], bank[7][:, 0:WIN]

        def chunks(eng, one):
            one(0, 0, 0)
            one(1, 1, 1)
            with eng.Fori(1, LAST // 2) as i:
                for u in range(2):
                    one(2 * i + u, u, 2)
            one(LAST, 0, 2)

        with nc.Block() as block:
            @block.sync
            def _(sp):
                def one(c, u, past):
                    start = TAIL0 if c is LAST else c * CH
                    if past == 2:
                        sp.wait_ge(onehot_ready, (c - 1) * NG)
                    sp.dma_start(idx[:, u, :], t["src"][bass.ds(start, CH)].rearrange("(p t) -> p t", t=T)).then_inc(idx_in[u], 16)
                    if past == 2:
                        sp.wait_ge(aT_ps, (c - 1) * NG)
                    sp.dma_start(a_sb[:, u, :, :], t["attr"][bass.ds(start, CH), :].rearrange("(p t) d -> p t d", t=T)).then_inc(a_in[u], 16)
                chunks(sp, one)

            @block.gpsimd
            def _(pool):
                def one(c, u, past):
                    pool.wait_ge(idx_in[u], (c - u) * 8 + 16)
                    if past == 2:
                        pool.wait_ge(summed, (c - 1) * NG)
                        pool.sem_inc(slot_free, 1)
                    for j in range(T):
                        nc.gpsimd.indirect_dma_start(
                            out=edge_rows[:, u, j, 0:ROW], out_offset=None, in_=table,
                            in_offset=bass.IndirectOffsetOnAxis(ap=idx[:, u, j:j + 1], axis=0)).then_inc(gathered[u][j // GT], 16)
                chunks(pool, one)
                for u in range(2):
                    for g in range(NG):
                        pool.wait_ge(gathered[u][g], (LAST // 2 + 1 - u) * GT * 16)
                nc.gpsimd.dma_reset()

            @block.tensor
            def _(pe):
                def edge_mlp(q, slot, first):
                    pe.wait_ge(aT_ready, q + 1)
                    if not first:
                        pe.wait_ge(r_ready, q)
                    for odd in range(2):
                        nc.tensor.matmul(z_bank[odd][:, :], ones_bf[:, :], bias_split[:, 0, :], start=True, stop=False)
                    for j in range(GP):
                        for odd in range(2):
                            half = slice(odd * ED, odd * ED + ED)
                            mm = nc.tensor.matmul(z_bank[odd][:, j * D:(j + 1) * D], aT[half, slot, j, :],
                                                  w1e[half, :], start=False, stop=j == GP - 1)
                    mm.then_inc(z_ps, 1)

                def sum_group(c, u, g, first):
                    q = c * NG + g
                    pe.wait_ge(onehot_ready, q + 1)
                    pe.wait_ge(r_ready, q + 1)
                    if g == 0 and not first:
                        pe.wait_ge(win_ready, c - 1)
                    for j in range(GT):
                        k = g * GT + j
                        mm = nc.tensor.matmul(sum_bank[u], onehot[:, g % 2, j, :], edge_rows[:, u, k, 1:XW],
                                              start=k == 0, stop=k == T - 1)
                    mm.then_inc(summed, 1)

                def turn_relu(c):
                    pe.wait_ge(win_ready, c + 1)
                    nc.tensor.transpose(rT_bank, win_sb[:, D:2 * D], ident[:, :]).then_inc(rT_ps, 1)

                def window(c, first):
                    pe.wait_ge(rT_ready, c + 1)
                    if not first:
                        pe.wait_ge(added, c)
                    nc.tensor.matmul(win_bank, w2e[:, :], rT_sb[:, :], start=True, stop=False)
                    nc.tensor.matmul(win_bank, win_sb[:, 0:D], ident[:, :], start=False, stop=True).then_inc(win_ps, 1)

                def one(c, u, past):
                    for g in range(NG):
                        q = c * NG + g
                        if g == 0:
                            pe.wait_ge(a_in[u], (c - u) * 8 + 16)
                        if not (past == 0 and g < 2):
                            pe.wait_ge(aT_ready, q - 1)
                        for j in range(GP):
                            k = g * GT + 2 * j
                            mm = nc.tensor.transpose(aT_bank[g % 2][:, j * 128:(j + 1) * 128],
                                                     a_sb[:, u, k:k + 2, :].rearrange("p j d -> p (j d)"), ident[:, :])
                        mm.then_inc(aT_ps, 1)
                        if not (past == 0 and g == 0):
                            edge_mlp(q - 1, (g + 1) % 2, past == 0)
                        if past >= 1:
                            sum_group(c - 1, 1 - u, g, past < 2)
                        if past == 2 and g == 0:
                            turn_relu(c - 2)
                        if past == 2 and g == 1:
                            window(c - 2, False)
                one(0, 0, 0)
                one(1, 1, 1)
                with pe.Fori(1, LAST // 2) as i:
                    for u in range(2):
                        one(2 * i + u, u, 2)
                one(LAST, 0, 2)
                edge_mlp(NC * NG - 1, 1, False)
                for g in range(NG):
                    sum_group(LAST, 0, g, False)
                    if g == 0:
                        turn_relu(LAST - 1)
                window(LAST - 1, False)
                turn_relu(LAST)
                window(LAST, False)

            @block.scalar
            def _(act):
                def relu(c, u, g, free):
                    act.wait_ge(z_ps, c * NG + g + 1)
                    if g == 0 and free:
                        act.wait_ge(summed, (c - 1) * NG)
                    for odd in range(2):
                        ins = nc.scalar.activation(
                            edge_rows[:, u, g * GT + odd:(g + 1) * GT:2, ROW:XW],
                            z_bank[odd][:, :].rearrange("p (j d) -> p j d", d=D), ACT.Relu)
                    ins.then_inc(r_ready, 1)

                def one(c, u, past):
                    for g in range(NG):
                        q = c * NG + g
                        act.wait_ge(aT_ps, q + 1)
                        if not (past == 0 and g < 2):
                            act.wait_ge(z_ps, q - 1)
                        nc.scalar.activation(aT[:, g % 2, :, :],
                                             aT_bank[g % 2][:, :].rearrange("p (j n) -> p j n", n=128),
                                             ACT.Copy).then_inc(aT_ready, 1)
                        if g > 0:
                            relu(c, u, g - 1, past == 2)
                        elif past >= 1:
                            relu(c - 1, 1 - u, NG - 1, False)
                chunks(act, one)
                relu(LAST, 0, NG - 1, False)

            @block.vector
            def _(v):
                def read_sums(c, u):
                    v.wait_ge(summed, (c + 1) * NG)
                    nc.vector.tensor_copy(win_sb[:, :], sum_bank[u]).then_inc(win_ready, 1)

                def read_rT(c):
                    v.wait_ge(rT_ps, c + 1)
                    nc.vector.tensor_copy(rT_sb[:, :], rT_bank).then_inc(rT_ready, 1)

                def add_window(c, first):
                    base = v.value_load(base_i[0:1, c:c + 1] if isinstance(c, int) else base_i[0:1, bass.ds(c, 1)],
                                        min_val=0, max_val=N - 1)
                    v.wait_ge(win_ps, c + 1)
                    if not first:
                        v.wait_ge(added, c)
                    nc.vector.tensor_tensor(acc[:, bass.ds(base, WIN)], acc[:, bass.ds(base, WIN)], win_bank,
                                            ALU.add).then_inc(added, 1)

                nc.vector.tensor_copy(base_i[:, :], base_f[:, :]).then_inc(starts_ready, 1)
                v.wait_ge(starts_ready, 1)

                def one(c, u, past):
                    if past == 2:
                        add_window(c - 2, False)
                    for g in range(NG):
                        v.wait_ge(gathered[u][g], (c - u) * (8 * GT) + 16 * GT)
                        q = c * NG + g
                        if not (past == 0 and g < 2):
                            v.wait_ge(summed, q - 1)
                        for j in range(GT):
                            k = g * GT + j
                            s_edge = edge_rows[:, u, k, 0:1]
                            ins = nc.vector.tensor_scalar(onehot[:, g % 2, j, :], iota[:, :],
                                                          rel[:, k, bass.ds(c, 1)], s_edge, ALU.is_equal, ALU.mult)
                        ins.then_inc(onehot_ready, 1)
                        if past >= 1 and g == 0:
                            read_sums(c - 1, 1 - u)
                        if past >= 1 and g == 1:
                            read_rT(c - 1)
                one(0, 0, 0)
                one(1, 1, 1)
                with v.Fori(1, LAST // 2) as i:
                    for u in range(2):
                        one(2 * i + u, u, 2)
                one(LAST, 0, 2)
                add_window(LAST - 1, False)
                read_sums(LAST, 0)
                read_rT(LAST)
                add_window(LAST, False)
                nc.vector.tensor_scalar(base_f[:, :], base_f[:, :], float(WIN), None, ALU.add)
                nc.vector.tensor_scalar(rel[:, :, :], rel[:, :, :], float(-WIN), None, ALU.add)

        clear(nc, every)


def kernel(**inputs):
    import numpy as _np
    import concourse.bacc as _bacc
    from concourse import mybir as _mybir
    from concourse.bass_utils import run_bass_kernel_spmd as _run

    nc = _bacc.Bacc("TRN2", target_bir_lowering=False, num_devices=1)
    layout = {
        "x": ("x", (N, D)), "src": ("src", (E,)), "dst": ("dst", (E,)), "attr": ("edge_attr_64", (E, ED)),
        "W1n": ("L0_gnn_W1n", (D, D)), "b1n": ("L0_gnn_b1n", (1, D)), "W2n": ("L0_gnn_W2n", (D, D)),
        "b2n": ("L0_gnn_b2n", (1, D)), "W1e": ("L0_gnn_W1e", (ED, D)), "b1e": ("L0_gnn_b1e", (1, D)),
        "W2e": ("L0_gnn_W2e", (D, D)), "b2e": ("L0_gnn_b2e", (1, D)), "eps": ("L0_gnn_gin_eps", (1, 1)),
        "rms_w": ("L0_gnn_rms_w", (1, D)),
    }
    arrays, t = {}, {}
    for name, (given, shape) in layout.items():
        a = _np.ascontiguousarray(inputs[given]).reshape(shape)
        arrays[f"in_{name}"] = a
        t[name] = nc.dram_tensor(f"in_{name}", shape, _mybir.dt.from_np(a.dtype), kind="ExternalInput").ap()
    t["out"] = nc.dram_tensor("out", (N, D), F32, kind="ExternalOutput").ap()
    build(nc, t)
    r = _run(nc, [arrays], core_ids=[0])
    return r.results[0]["out"]
```
